# Optimizing a Trainium2 kernel written in Bass

```python
import numpy as np
import jax
import jax.numpy as jnp

def _softmax(x, axis=-1):
    return jax.nn.softmax(x, axis=axis)

def _gelu(x):
    return jax.nn.gelu(x, approximate=True)

def _silu(x):
    return jax.nn.silu(x)

def _sigmoid(x):
    return jax.nn.sigmoid(x)

def _layernorm(x, axis=-1, eps=1e-05):
    m = jnp.mean(x, axis=axis, keepdims=True)
    v = jnp.var(x, axis=axis, keepdims=True)
    return (x - m) / jnp.sqrt(v + eps)

def _scatter_add(tgt, idx, src, axis=0):
    return tgt.at[idx].add(src)

def _segment_sum(src, seg, n):
    return jax.ops.segment_sum(src, seg, n)
kernel_name = 'mk_hybrid_d1_jaxref_r4_fc7ed8'

def setup_inputs(seed: int=0):
    np.random.seed(seed)
    _w = jnp.asarray

    def _L0_attn_a_setup():
        import math
        import jax, jax.numpy as jnp
        import numpy as np
        B, T, E, H = (1, 512, 512, 16)
        D = E // H // 2
        DEPTH = 12
        LAMBDA_INIT = 0.8 - 0.6 * math.exp(-0.3 * DEPTH)
        EPS = 1e-05
        NEG = -1e+30

        def rotary_cos_sin(seqlen, dim):
            inv_freq = 1.0 / 10000.0 ** (jnp.arange(0, dim, 2, dtype=jnp.float32) / dim)
            t = jnp.arange(seqlen, dtype=jnp.float32)
            freqs = jnp.outer(t, inv_freq)
            return (jnp.cos(freqs), jnp.sin(freqs))

        def apply_rotary_interleaved(x, cos, sin):
            x1 = x[..., 0::2]
            x2 = x[..., 1::2]
            c = cos[None, :, None, :]
            s = sin[None, :, None, :]
            o1 = x1 * c - x2 * s
            o2 = x1 * s + x2 * c
            return jnp.stack([o1, o2], axis=-1).reshape(x.shape)

        def causal_attn_pair(q, k, v1, v2, mask, scale):
            s = jnp.einsum('bthd,bshd->bhts', q, k) * scale
            s = jnp.where(mask, s, NEG)
            a = jax.nn.softmax(s, axis=-1)
            o1 = jnp.einsum('bhts,bshd->bthd', a, v1)
            o2 = jnp.einsum('bhts,bshd->bthd', a, v2)
            return jnp.concatenate([o1, o2], axis=-1)
        key = jax.random.key(seed)
        ks = jax.random.split(key, 10)
        return {'query': jax.random.normal(ks[0], (B, T, E), dtype=jnp.float32), 'Wq': jax.random.normal(ks[1], (E, E), dtype=jnp.float32) * 0.02, 'Wk': jax.random.normal(ks[2], (E, E), dtype=jnp.float32) * 0.02, 'Wv': jax.random.normal(ks[3], (E, E), dtype=jnp.float32) * 0.02, 'Wout': jax.random.normal(ks[4], (E, E), dtype=jnp.float32) * 0.02, 'lambda_q1': jax.random.normal(ks[5], (D,), dtype=jnp.float32) * 0.1, 'lambda_k1': jax.random.normal(ks[6], (D,), dtype=jnp.float32) * 0.1, 'lambda_q2': jax.random.normal(ks[7], (D,), dtype=jnp.float32) * 0.1, 'lambda_k2': jax.random.normal(ks[8], (D,), dtype=jnp.float32) * 0.1, 'rms_weight': jnp.ones((2 * D,), dtype=jnp.float32)}
    _L0_attn_a_in = _L0_attn_a_setup()

    def _L0_attn_b_setup():
        import jax, jax.numpy as jnp
        import numpy as np
        B, S, D = (4, 1024, 512)
        THETA = 10000.0
        LN_EPS = 1e-05

        def _layernorm(x, w, b):
            mu = jnp.mean(x, axis=-1, keepdims=True)
            var = jnp.mean(jnp.square(x - mu), axis=-1, keepdims=True)
            return (x - mu) * jax.lax.rsqrt(var + LN_EPS) * w + b

        def _rope_half(x):
            rot_dim = x.shape[-1] // 2
            seq = x.shape[-2]
            inv_freq = 1.0 / THETA ** (jnp.arange(0, rot_dim, 2, dtype=jnp.float32) / rot_dim)
            freqs = jnp.arange(seq, dtype=jnp.float32)[:, None] * inv_freq[None, :]
            freqs = jnp.repeat(freqs, 2, axis=-1)
            cos, sin = (jnp.cos(freqs), jnp.sin(freqs))
            xl, xr = (x[..., :rot_dim], x[..., rot_dim:])
            x1, x2 = (xl[..., 0::2], xl[..., 1::2])
            rh = jnp.stack((-x2, x1), axis=-1).reshape(xl.shape)
            return jnp.concatenate([xl * cos + rh * sin, xr], axis=-1)

        def _cos_sim(x):
            return x / jnp.linalg.norm(x, axis=-1, keepdims=True)
        key = jax.random.key(seed)
        k0, k1, k2 = jax.random.split(key, 3)
        X = jax.random.normal(k0, (B, S, D), jnp.float32)
        ln_w = jnp.ones((D,), jnp.float32)
        ln_b = jnp.zeros((D,), jnp.float32)
        W_in = jax.random.normal(k1, (D, 3 * D), jnp.float32) * D ** (-0.5)
        b_in = jnp.zeros((3 * D,), jnp.float32)
        W_out = jax.random.normal(k2, (D, D), jnp.float32) * D ** (-0.5)
        b_out = jnp.zeros((D,), jnp.float32)
        return {'X': X, 'ln_w': ln_w, 'ln_b': ln_b, 'W_in': W_in, 'b_in': b_in, 'W_out': W_out, 'b_out': b_out}
    _L0_attn_b_in = _L0_attn_b_setup()

    def _L0_ffn_setup():
        import jax, jax.numpy as jnp
        import numpy as np
        H = 512
        E = 8
        K = 2
        I = 16
        key = jax.random.key(seed)
        k1, k2, k3, k4 = jax.random.split(key, 4)
        B, T = (2, 1024)
        x = jax.random.normal(k1, (B, T, H), dtype=jnp.float32)
        router_w = jax.random.normal(k2, (E, H), dtype=jnp.float32) / np.sqrt(H)
        down_w = jax.random.normal(k3, (E, I, H), dtype=jnp.float32) / np.sqrt(H)
        up_w = jax.random.normal(k4, (E, H, I), dtype=jnp.float32) / np.sqrt(I)
        return {'x': x, 'router_w': router_w, 'down_w': down_w, 'up_w': up_w}
    _L0_ffn_in = _L0_ffn_setup()
    _d = {'L0_attn_a_query': _L0_attn_a_in['query'], 'L0_attn_a_Wq': _L0_attn_a_in['Wq'], 'L0_attn_a_Wk': _L0_attn_a_in['Wk'], 'L0_attn_a_Wv': _L0_attn_a_in['Wv'], 'L0_attn_a_Wout': _L0_attn_a_in['Wout'], 'L0_attn_a_lambda_q1': _L0_attn_a_in['lambda_q1'], 'L0_attn_a_lambda_k1': _L0_attn_a_in['lambda_k1'], 'L0_attn_a_lambda_q2': _L0_attn_a_in['lambda_q2'], 'L0_attn_a_lambda_k2': _L0_attn_a_in['lambda_k2'], 'L0_attn_a_rms_weight': _L0_attn_a_in['rms_weight'], 'L0_attn_b_ln_w': _L0_attn_b_in['ln_w'], 'L0_attn_b_ln_b': _L0_attn_b_in['ln_b'], 'L0_attn_b_W_in': _L0_attn_b_in['W_in'], 'L0_attn_b_b_in': _L0_attn_b_in['b_in'], 'L0_attn_b_W_out': _L0_attn_b_in['W_out'], 'L0_attn_b_b_out': _L0_attn_b_in['b_out'], 'L0_ffn_router_w': _L0_ffn_in['router_w'], 'L0_ffn_down_w': _L0_ffn_in['down_w'], 'L0_ffn_up_w': _L0_ffn_in['up_w']}
    _x0 = _d['L0_attn_a_query']
    _d['L0_attn_a_query'] = jax.random.normal(jax.random.fold_in(jax.random.key(seed), 1), (2, 1024, 512), dtype=_x0.dtype)
    del _x0
    return _d

def reference(L0_attn_a_query, L0_attn_a_Wq, L0_attn_a_Wk, L0_attn_a_Wv, L0_attn_a_Wout, L0_attn_a_lambda_q1, L0_attn_a_lambda_k1, L0_attn_a_lambda_q2, L0_attn_a_lambda_k2, L0_attn_a_rms_weight, L0_attn_b_ln_w, L0_attn_b_ln_b, L0_attn_b_W_in, L0_attn_b_b_in, L0_attn_b_W_out, L0_attn_b_b_out, L0_ffn_router_w, L0_ffn_down_w, L0_ffn_up_w):

    def _L0_attn_a_ref(query, Wq, Wk, Wv, Wout, lambda_q1, lambda_k1, lambda_q2, lambda_k2, rms_weight):
        import math
        import jax, jax.numpy as jnp
        import numpy as np
        B, T, E, H = (1, 512, 512, 16)
        D = E // H // 2
        DEPTH = 12
        LAMBDA_INIT = 0.8 - 0.6 * math.exp(-0.3 * DEPTH)
        EPS = 1e-05
        NEG = -1e+30

        def rotary_cos_sin(seqlen, dim):
            inv_freq = 1.0 / 10000.0 ** (jnp.arange(0, dim, 2, dtype=jnp.float32) / dim)
            t = jnp.arange(seqlen, dtype=jnp.float32)
            freqs = jnp.outer(t, inv_freq)
            return (jnp.cos(freqs), jnp.sin(freqs))

        def apply_rotary_interleaved(x, cos, sin):
            x1 = x[..., 0::2]
            x2 = x[..., 1::2]
            c = cos[None, :, None, :]
            s = sin[None, :, None, :]
            o1 = x1 * c - x2 * s
            o2 = x1 * s + x2 * c
            return jnp.stack([o1, o2], axis=-1).reshape(x.shape)

        def causal_attn_pair(q, k, v1, v2, mask, scale):
            s = jnp.einsum('bthd,bshd->bhts', q, k) * scale
            s = jnp.where(mask, s, NEG)
            a = jax.nn.softmax(s, axis=-1)
            o1 = jnp.einsum('bhts,bshd->bthd', a, v1)
            o2 = jnp.einsum('bhts,bshd->bthd', a, v2)
            return jnp.concatenate([o1, o2], axis=-1)
        bsz, tgt_len, embed_dim = query.shape
        cos, sin = rotary_cos_sin(tgt_len, D)
        scale = D ** (-0.5)
        mask = jnp.tril(jnp.ones((tgt_len, tgt_len), dtype=bool))[None, None]
        q = (query @ Wq).reshape(bsz, tgt_len, 2 * H, D)
        k = (query @ Wk).reshape(bsz, tgt_len, 2 * H, D)
        v = (query @ Wv).reshape(bsz, tgt_len, H, 2, D)
        q = apply_rotary_emb = apply_rotary_interleaved(q, cos, sin)
        k = apply_rotary_interleaved(k, cos, sin)
        q = q.reshape(bsz, tgt_len, H, 2, D)
        k = k.reshape(bsz, tgt_len, H, 2, D)
        q1, q2 = (q[:, :, :, 0], q[:, :, :, 1])
        k1, k2 = (k[:, :, :, 0], k[:, :, :, 1])
        v1, v2 = (v[:, :, :, 0], v[:, :, :, 1])
        attn1 = causal_attn_pair(q1, k1, v1, v2, mask, scale)
        attn2 = causal_attn_pair(q2, k2, v1, v2, mask, scale)
        lambda_1 = jnp.exp(jnp.sum(lambda_q1 * lambda_k1))
        lambda_2 = jnp.exp(jnp.sum(lambda_q2 * lambda_k2))
        lambda_full = lambda_1 - lambda_2 + LAMBDA_INIT
        f1 = jnp.fft.rfft(attn1, axis=1)
        f2 = jnp.fft.rfft(attn2, axis=1)
        attn_freq = f1 - lambda_full * f2
        n_freq = attn_freq.shape[1]
        sigma = 0.3 / 2.0
        x = jnp.linspace(0.0, 1.0, n_freq)
        filt = jnp.exp(-0.5 * (x / sigma) ** 2)
        attn_freq = attn_freq * filt[None, :, None, None]
        attn = jnp.fft.irfft(attn_freq, n=tgt_len, axis=1)
        attn = attn * jax.lax.rsqrt(jnp.mean(attn * attn, axis=-1, keepdims=True) + EPS) * rms_weight
        attn = attn * (1.0 - LAMBDA_INIT)
        attn = attn.reshape(bsz, tgt_len, H * 2 * D)
        return attn @ Wout

    def _L0_attn_b_ref(X, ln_w, ln_b, W_in, b_in, W_out, b_out):
        import jax, jax.numpy as jnp
        import numpy as np
        B, S, D = (4, 1024, 512)
        THETA = 10000.0
        LN_EPS = 1e-05

        def _layernorm(x, w, b):
            mu = jnp.mean(x, axis=-1, keepdims=True)
            var = jnp.mean(jnp.square(x - mu), axis=-1, keepdims=True)
            return (x - mu) * jax.lax.rsqrt(var + LN_EPS) * w + b

        def _rope_half(x):
            rot_dim = x.shape[-1] // 2
            seq = x.shape[-2]
            inv_freq = 1.0 / THETA ** (jnp.arange(0, rot_dim, 2, dtype=jnp.float32) / rot_dim)
            freqs = jnp.arange(seq, dtype=jnp.float32)[:, None] * inv_freq[None, :]
            freqs = jnp.repeat(freqs, 2, axis=-1)
            cos, sin = (jnp.cos(freqs), jnp.sin(freqs))
            xl, xr = (x[..., :rot_dim], x[..., rot_dim:])
            x1, x2 = (xl[..., 0::2], xl[..., 1::2])
            rh = jnp.stack((-x2, x1), axis=-1).reshape(xl.shape)
            return jnp.concatenate([xl * cos + rh * sin, xr], axis=-1)

        def _cos_sim(x):
            return x / jnp.linalg.norm(x, axis=-1, keepdims=True)
        h = _layernorm(X, ln_w, ln_b)
        qkv = h @ W_in + b_in
        Q, K, V = jnp.split(qkv, 3, axis=-1)
        Q = _rope_half(Q)
        K = _rope_half(K)
        A = jnp.sum(_cos_sim(K) * V, axis=-2)
        Y = A[:, None, :] * Q
        Y = Y @ W_out + b_out
        return Y + X

    def _L0_ffn_ref(x, router_w, down_w, up_w):
        import jax, jax.numpy as jnp
        import numpy as np
        H = 512
        E = 8
        K = 2
        I = 16
        logits = jnp.einsum('bth,eh->bte', x, router_w)
        weights = jax.nn.softmax(logits, axis=-1)
        top_w, top_idx = jax.lax.top_k(weights, K)
        topk_mask = jnp.sum(jax.nn.one_hot(top_idx, E, dtype=x.dtype), axis=-2)
        gate = weights * topk_mask
        h = jnp.einsum('bth,eih->beti', x, down_w)
        a = jax.nn.silu(h)
        expert_out = jnp.einsum('beti,ehi->beth', a, up_w)
        out = jnp.einsum('beth,bte->bth', expert_out, gate)
        return out
    x = L0_attn_a_query
    x = x + _L0_attn_a_ref(_layernorm(x, axis=-1), L0_attn_a_Wq, L0_attn_a_Wk, L0_attn_a_Wv, L0_attn_a_Wout, L0_attn_a_lambda_q1, L0_attn_a_lambda_k1, L0_attn_a_lambda_q2, L0_attn_a_lambda_k2, L0_attn_a_rms_weight)
    x = x + _L0_ffn_ref(_layernorm(x, axis=-1), L0_ffn_router_w, L0_ffn_down_w, L0_ffn_up_w)
    x = x + _L0_attn_b_ref(_layernorm(x, axis=-1), L0_attn_b_ln_w, L0_attn_b_ln_b, L0_attn_b_W_in, L0_attn_b_b_in, L0_attn_b_W_out, L0_attn_b_b_out)
    x = x + _L0_ffn_ref(_layernorm(x, axis=-1), L0_ffn_router_w, L0_ffn_down_w, L0_ffn_up_w)
    return x

_drawn_inputs = setup_inputs


def setup_inputs(seed=0):
    import zlib

    import numpy as np

    out = dict(_drawn_inputs(seed))
    spreads = {'L0_attn_a_rms_weight': (1.0, 0.2),
     'L0_attn_b_ln_w': (1.0, 0.2),
     'L0_attn_b_ln_b': (0.0, 0.1),
     'L0_attn_b_b_in': (0.0, 0.1),
     'L0_attn_b_b_out': (0.0, 0.1)}
    factors = {'L0_attn_a_lambda_q1': 4.837, 'L0_attn_a_lambda_q2': 3.149, 'L0_attn_a_lambda_k2': 2.892}
    for name, (base, spread) in spreads.items():
        noise = np.random.default_rng([zlib.crc32(name.encode()), seed]).standard_normal(out[name].shape)
        drawn = base * np.exp(spread * noise) if base else spread * noise
        out[name] = jnp.asarray(drawn.astype(out[name].dtype))
    for name, factor in factors.items():
        out[name] = (out[name] * factor).astype(out[name].dtype)
    return out
```

```python
from contextlib import ExitStack

import numpy as np

import concourse.bass as bass
from concourse import mybir

F32 = mybir.dt.float32
BF16 = mybir.dt.bfloat16
ALU = mybir.AluOpType
ACT = mybir.ActivationFunctionType
AX = mybir.AxisListType

B, T, E = 2, 1024, 512
P = 128
NT = B * T // P
TB = T // P
KC = E // P
H = 16
D = E // H // 2
GH = 4
G = H // GH
NP = 2 * GH
HALF = T // 2
NX, IX = 8, 16
NROPE = E // 2
EPS = 1e-5
LAMBDA_INIT = 0.8 - 0.6 * float(np.exp(-0.3 * 12))
MASKED = -1e30
BAND = 32
PIECES = 6 * D
ROWS = PIECES + 3


class Step:

    def __init__(self, reg, c, stride, least=0):
        self.reg, self.c, self.stride, self.least = reg, c, stride, least

    def back(self, n):
        return Step(self.reg, self.c - n, self.stride, self.least)

    def exists(self, n):
        return self.reg is not None or 0 <= self.c < n

    def times(self, per, add=0):
        if self.reg is None:
            return self.c * per + add
        return self.reg * (self.stride * per) + (self.c * per + add)

    def reused(self, n):
        return self.reg is not None or self.c >= n

    @property
    def slot(self):
        return self.c % self.stride

    def round(self, per, add=0):
        if self.reg is None:
            return (self.c // self.stride) * per + add
        return self.reg * per + ((self.c // self.stride) * per + add)

    def past(self, n):
        if self.reg is None:
            return self.c - n >= 0
        assert self.stride * self.least + self.c >= n, (self.c, n)
        return True


def steps(eng, total, stride, first, last, body):
    for c in range(first):
        body(Step(None, c, stride))
    if total > first:
        with eng.Fori(first // stride, total // stride) as i:
            for c in range(stride):
                body(Step(i, c, stride, first // stride))
    for c in range(max(total, first), last):
        body(Step(None, c, stride))


def wait_alone(eng, sem, value, mark):
    eng.wait_ge(sem, value)
    if not isinstance(value, int):
        eng.sem_inc(mark, 1)


class Chain:

    def __init__(self, eng, sem, step, per, mark=None):
        self.eng, self.sem, self.step, self.per, self.n, self.mark = eng, sem, step, per, 0, mark

    def link(self, ins):
        self.n += 1
        ins.then_inc(self.sem, 1)
        value = self.step.times(self.per, self.n)
        if self.mark:
            wait_alone(self.eng, self.sem, value, self.mark)
        else:
            self.eng.wait_ge(self.sem, value)

    def end(self):
        assert self.n == self.per, (self.n, self.per)



def shape_constants():
    f = np.float32
    bf = mybir.dt.np(BF16)
    inv = (f(1.0) / f(10000.0) ** (np.arange(0, D, 2, dtype=f) / f(D))).astype(f)
    ang = np.outer(np.arange(T, dtype=f), inv).astype(f)
    sign = np.where(np.arange(P) % 2 == 0, -1.0, 1.0).astype(f)
    rows = (np.arange(P) % D) // 2
    cos_a = np.cos(ang).astype(f).T[rows]
    sin_a = np.sin(ang).astype(f).T[rows] * sign[:, None]
    inv_b = (f(1.0) / f(10000.0) ** (np.arange(0, NROPE, 2, dtype=f) / f(NROPE))).astype(f)
    ang_b = np.repeat((np.arange(T, dtype=f)[:, None] * inv_b[None, :]).astype(f), 2, axis=-1)
    sgn = np.where(np.arange(NROPE) % 2 == 0, -1.0, 1.0).astype(f)
    rope_b = np.concatenate([np.cos(ang_b), np.sin(ang_b) * sgn], axis=1).astype(f)
    filt = np.exp(-0.5 * (np.linspace(0.0, 1.0, T // 2 + 1) / 0.15) ** 2)
    taps = np.fft.irfft(filt, n=T)
    u = np.arange(P + 2 * BAND)[None, :] - BAND - np.arange(P)[:, None]
    near = np.where(np.abs(u) <= BAND, taps[u % T], 0.0).astype(f)
    u = np.arange(3 * HALF)[None, :] - np.arange(P)[:, None]
    dist = np.minimum(u % T, (-u) % T)
    far = np.where(dist > BAND, taps[u % T], 0.0).astype(bf)
    i = np.arange(P)
    ident = np.eye(P, dtype=f)
    mask_s = np.where(i[None, :] > i[:, None], MASKED, 0.0).astype(bf)
    mask_t = np.ascontiguousarray(mask_s.T)
    heads = (i[:, None] // (2 * D) == i[None, :] // (2 * D)).astype(f) / (2 * D)
    tri = (np.arange(NX)[None, :] < np.arange(NX)[:, None]).astype(f).reshape(1, NX * NX)
    tri = np.broadcast_to(tri, (P, NX * NX)).copy()
    which = np.zeros((P, NT, B), f)
    which[:, np.arange(NT), np.arange(NT) // TB] = 1.0
    return {
        "c_cos": cos_a, "c_sin": sin_a, "c_rope": rope_b, "c_near": near, "c_far": far, "c_ident": ident,
        "c_identb": ident.astype(bf), "c_mask_s": mask_s, "c_mask_t": mask_t, "c_heads": heads,
        "c_tri": tri, "c_which": which.reshape(P, NT * B),
    }


def build(nc, a, out):
    x_tiles = a["query"].rearrange("b (n p) e -> (b n) p e", p=P)
    out_tiles = out.rearrange("b (n p) e -> (b n) p e", p=P)
    v_scr = nc.dram_tensor("v_scratch", (NT, P, E), F32, kind="Internal").ap()
    piece_scr = nc.dram_tensor("piece_scratch", (2, 2, 3, P, T), BF16, kind="Internal").ap()
    shift_scr = nc.dram_tensor("shift_scratch", (2, 3, NP, HALF), BF16, kind="Internal").ap()
    att_scr = nc.dram_tensor("att_scratch", (B * G, P, T), F32, kind="Internal").ap()
    qt_scr = nc.dram_tensor("qt_scratch", (NT, P, KC, P), F32, kind="Internal").ap()
    res_scr = nc.dram_tensor("res_scratch", (NT, P, E), F32, kind="Internal").ap()
    with ExitStack() as ctx:
        def sb(name, shape, dt=F32):
            return ctx.enter_context(nc.sbuf_tensor(name, shape, dt))
        ident = sb("ident", [P, P])
        xnT = sb("xnT", [P, KC, NT * P])
        normalise(nc, a, x_tiles, v_scr, ident, xnT)
        attention(nc, a, v_scr, piece_scr, shift_scr, att_scr, ident, xnT)
    with ExitStack() as ctx:
        def sb(name, shape, dt=F32):
            return ctx.enter_context(nc.sbuf_tensor(name, shape, dt))
        w = dict(
            ident=sb("ident2", [P, P]), tri=sb("tri", [P, NX, NX]),
            down=sb("down", [P, KC, NX * IX + NX]), up=sb("up", [P, E]),
            wab=sb("wab", [P, B, KC, E]), bout=sb("bout", [P, E]),
        )
        middle(nc, a, x_tiles, att_scr, qt_scr, res_scr, w)
        last(nc, a, out_tiles, qt_scr, res_scr, w)



def normalise(nc, a, x_tiles, v_scr, ident, xnT):
    R = 4
    with ExitStack() as ctx:
        def sb(name, shape, dt=F32):
            return ctx.enter_context(nc.sbuf_tensor(name, shape, dt))

        def sem(name):
            return ctx.enter_context(nc.semaphore(name))
        mark_sp, mark_pool, mark_dve = (sem(f"n_mark_{e}") for e in ("sp", "pool", "dve"))
        wv = sb("wv", [P, KC, E])
        x = sb("x1in", [P, R, E])
        xn = sb("xn", [P, R, E])
        st = sb("st", [P, R, 6])
        mv = sb("mv", [P, R, 2])
        rstd = sb("rstd", [P, R, 1])
        mhalf = sb("mhalf", [P, 1])
        xt = sb("xt", [P, R, KC, P])
        v = sb("v", [P, R, E])
        tp = [ctx.enter_context(nc.psum_tensor(f"n_tp{i}", [P, E], F32)) for i in range(R)]
        vp = [ctx.enter_context(nc.psum_tensor(f"n_vp{i}", [P, E], F32)) for i in range(R)]
        s_const, s_mhalf, s_var = sem("n_const"), sem("n_mhalf"), sem("n_var")
        s_x = [sem(f"n_x{i}") for i in range(R)]
        s_stat, s_agg, s_rstd, s_xn = sem("n_stat"), sem("n_agg"), sem("n_rstd"), sem("n_xn")
        s_tp, s_xt, s_big, s_vp, s_v = sem("n_tp"), sem("n_xt"), sem("n_big"), sem("n_vp"), sem("n_v")
        s_vout = [sem(f"n_vout{i}") for i in range(R)]
        block = ctx.enter_context(nc.Block())

        @block.sync
        def _(sp):
            sp.dma_start(wv[:], a["Wv"].rearrange("(c p) n -> p c n", p=P)).then_inc(s_const, 16)
            sp.dma_start(ident[:], a["c_ident"]).then_inc(s_const, 16)

            def body(t):
                if t.past(R):
                    wait_alone(sp, s_xn, t.times(1, 1 - R), mark_sp)
                sp.dma_start(x[:, t.slot], x_tiles[bass.ds(t.times(1), 1)].rearrange("a p e -> p (a e)"))\
                    .then_inc(s_x[t.slot], 16)
            steps(sp, NT, R, 2 * R, NT, body)

        @block.vector
        def _(dve):
            def body(s):
                t = s
                if t.exists(NT):
                    dve.wait_ge(s_x[t.slot], t.round(16, 16))
                    nc.vector.bn_stats(st[:, t.slot], x[:, t.slot]).then_inc(s_stat, 1)
                    wait_alone(dve, s_stat, t.times(1, 1), mark_dve)
                    nc.vector.bn_aggr(mv[:, t.slot], st[:, t.slot]).then_inc(s_agg, 1)
                t = s.back(1)
                if t.exists(NT):
                    dve.wait_ge(s_rstd, t.times(1, 1))
                    if t.past(R):
                        dve.wait_ge(s_tp, t.times(1, 1 - R))
                    nc.vector.tensor_scalar(xn[:, t.slot], x[:, t.slot], mv[:, t.slot, 0:1], rstd[:, t.slot],
                                            ALU.subtract, ALU.mult).then_inc(s_xn, 1)
                t = s.back(2)
                if t.exists(NT):
                    dve.wait_ge(s_tp, t.times(1, 1))
                    if t.past(3):
                        dve.wait_ge(s_vp, t.times(1, -2))
                        dve.wait_ge(s_big, t.times(1, -2))
                    nc.vector.tensor_copy(xt[:, t.slot], tp[t.slot][:].rearrange("p (c t) -> p c t", c=KC))\
                        .then_inc(s_xt, 1)
            steps(dve, NT, R, 2 * R, NT + 2, body)

        @block.gpsimd
        def _(pool):
            nc.gpsimd.memset(mhalf[:], -0.5).then_inc(s_mhalf, 1)
            pool.wait_ge(s_mhalf, 1)

            def body(s):
                t = s
                if t.exists(NT):
                    wait_alone(pool, s_agg, t.times(1, 1), mark_pool)
                    if t.past(R):
                        wait_alone(pool, s_xn, t.times(1, 1 - R), mark_pool)
                    nc.gpsimd.tensor_scalar(rstd[:, t.slot], mv[:, t.slot, 1:2], EPS, None, ALU.add).then_inc(s_var, 1)
                    wait_alone(pool, s_var, t.times(1, 1), mark_pool)
                    nc.gpsimd.tensor_tensor(rstd[:, t.slot], rstd[:, t.slot], mhalf[:], ALU.pow).then_inc(s_rstd, 1)
                t = s.back(2)
                if t.exists(NT):
                    wait_alone(pool, s_xt, t.times(1, 1), mark_pool)
                    nc.gpsimd.tensor_copy(xnT[:, :, bass.ds(t.times(P), P)], xt[:, t.slot]).then_inc(s_big, 1)
            steps(pool, NT, R, 2 * R, NT + 2, body)

        @block.tensor
        def _(pe):
            pe.wait_ge(s_const, 32)

            def body(s):
                t = s.back(1)
                if t.exists(NT):
                    pe.wait_ge(s_xn, t.times(1, 1))
                    if t.past(R):
                        pe.wait_ge(s_xt, t.times(1, 1 - R))
                    for c in range(KC):
                        mm = nc.tensor.transpose(tp[t.slot][:, c * P:(c + 1) * P], xn[:, t.slot, c * P:(c + 1) * P],
                                                 ident[:])
                    mm.then_inc(s_tp, 1)
                t = s.back(2)
                if t.exists(NT):
                    pe.wait_ge(s_xt, t.times(1, 1))
                    if t.past(3):
                        pe.wait_ge(s_v, t.times(1, -2))
                    for c in range(KC):
                        mm = nc.tensor.matmul(vp[t.slot][:], xt[:, t.slot, c], wv[:, c], start=(c == 0),
                                              stop=(c == KC - 1))
                    mm.then_inc(s_vp, 1)
            steps(pe, NT, R, 2 * R, NT + 2, body)

        @block.scalar
        def _(act):
            def body(s):
                t = s.back(2)
                if t.exists(NT):
                    act.wait_ge(s_vp, t.times(1, 1))
                    if t.reused(R):
                        act.wait_ge(s_vout[t.slot], t.round(16))
                    nc.scalar.copy(v[:, t.slot], vp[t.slot][:]).then_inc(s_v, 1)
                    act.wait_ge(s_v, t.times(1, 1))
                    act.dma_start(v_scr[bass.ds(t.times(1), 1)].rearrange("a p e -> p (a e)"), v[:, t.slot])\
                        .then_inc(s_vout[t.slot], 16)
            steps(act, NT, R, 2 * R, NT + 2, body)
            for i in range(R):
                act.wait_ge(s_vout[i], 16 * (NT // R))



def near_windows(half):
    found = []
    for j in range(TB):
        lo, hi = j * P - BAND, (j + 1) * P + BAND
        for wrap in (-T, 0, T):
            s, e = max(lo + wrap, half * HALF), min(hi + wrap, (half + 1) * HALF)
            if s < e:
                found.append((j, s - wrap - lo, s - half * HALF, e - s))
    return found


def rows_units():
    units = []
    for i in range(TB):
        n = 2 if (i + 1) * P <= HALF else 1
        units += [(i, a, n) for a in range(0, NP, n)]
    return units


def prob_units():
    return [(h, j, w, g) for h in range(2) for j in range((h + 1) * TB // 2) for w in range(2) for g in (0, 2)]


LOWPASS_AT = {2: "turn0", 5: "turn1", 9: "low0", 12: "low1", 15: "square0", 18: "square1"}
PROJECT_AT = {21: "q0", 24: "q1", 28: "k0", 31: "k1"}
SHIFT0_AT, SHIFT1_AT = 26, 6
ROOT_AT = {20: 0, 24: 1}
NSLOT = 3
NPROB = 4


def attention(nc, a, v_scr, piece_scr, shift_scr, att_scr, ident, xnT):
    NG = B * G
    RU, PU = rows_units(), prob_units()
    NU, NQ = len(RU), len(PU)
    UN = NU + NQ
    NV = NQ // 2
    SH = 4
    with ExitStack() as ctx:
        def sb(name, shape, dt=F32):
            return ctx.enter_context(nc.sbuf_tensor(name, shape, dt))

        def sem(name):
            return ctx.enter_context(nc.semaphore(name))
        mark_sp, mark_pool, mark_dve = (sem(f"a_mark_{e}") for e in ("sp", "pool", "dve"))
        cos, sin = sb("cos", [P, T]), sb("sin", [P, T])
        near = sb("near", [P, P + 2 * BAND])
        far = sb("far", [P, 3 * HALF], BF16)
        identb = sb("identb", [P, P], BF16)
        mask_s, mask_t = sb("mask_s", [P, P], BF16), sb("mask_t", [P, P], BF16)
        headsum = sb("headsum", [P, P])
        lam_in = sb("lam_in", [P, 4, D])
        lam_p = sb("lam_p", [P, 2, D])
        lam_e = sb("lam_e", [P, 2, 1])
        nlam = sb("nlam", [P, 1])
        wg = sb("wg", [P, 2, KC, 2, P])
        vg = sb("vg", [P, 2, TB, P])
        vn = sb("vn", [P, 2, TB, P])
        qst, kst = sb("qst", [P, 2, NP, T], BF16), sb("kst", [P, 2, NP, T], BF16)
        raw = sb("raw", [P, 2, T])
        swapped = sb("swapped", [P, 2, T])
        rot = sb("rot", [P, T])
        pieces = sb("pieces", [P, 2, 3, T], BF16)
        prob = sb("prob", [P, NPROB, 2, HALF])
        nmax, den = sb("nmax", [P, NP, TB]), sb("den", [P, NP, TB])
        shift, rest = sb("shift", [P, NP, TB]), sb("rest", [P, NP, TB])
        shp = sb("shp", [P, TB, 3, NP], BF16)
        shrow = sb("shrow", [3 * NP, 2, HALF], BF16)
        oT = sb("oT", [P, T])
        onat = sb("onat", [P, TB, P])
        onb = sb("onb", [P, TB, P], BF16)
        y = sb("y", [P, T])
        sq = sb("sq", [P, T])
        rs = sb("rs", [P, HALF])
        newton = sb("newton", [P, HALF])

        score = [ctx.enter_context(nc.psum_tensor(f"score{i}", [P, 2, HALF], F32)) for i in range(NSLOT)]
        acc = ctx.enter_context(nc.psum_tensor("acc", [P, HALF], F32))
        misc = ctx.enter_context(nc.psum_tensor("misc", [P, HALF], F32))
        miscb = misc[:].bitcast(BF16)

        s_const, s_lam = sem("a_const"), sem("a_lam")
        s_wg = [sem(f"a_wg{i}") for i in range(2)]
        s_vg = [sem(f"a_vg{i}") for i in range(2)]
        s_vn = sem("a_vn")
        s_slot, s_max, s_exp = sem("a_slot"), sem("a_max"), sem("a_exp")
        s_misc, s_mread = sem("a_misc"), sem("a_mread")
        s_swap, s_cosm, s_rot, s_chain, s_pc = sem("a_swap"), sem("a_cosm"), sem("a_rot"), sem("a_chain"), sem("a_pc")
        s_piece = [sem(f"a_piece{i}") for i in range(2)]
        s_stack = [[sem(f"a_stack{w}{i}") for i in range(2)] for w in range(2)]
        s_ln, s_sh, s_shrow = sem("a_ln"), sem("a_sh"), sem("a_shrow")
        s_shdma = [sem(f"a_shdma{h}") for h in range(2)]
        s_shout = [sem(f"a_shout{h}") for h in range(2)]
        s_pv, s_oT, s_ones = sem("a_pv"), sem("a_oT"), sem("a_ones")
        s_nat, s_y, s_sq, s_rs, s_att = sem("a_nat"), sem("a_y"), sem("a_sq"), sem("a_rs"), sem("a_att")
        s_newton = sem("a_newton")
        s_attdma = sem("a_attdma")
        block = ctx.enter_context(nc.Block())

        order = [LOWPASS_AT[n] for n in sorted(LOWPASS_AT)]
        order += [u for n, u in sorted(list(PROJECT_AT.items()) + [(SHIFT0_AT, "shift0")])] + ["shift1"]
        NM = len(order)

        def use(g, name):
            return g.times(NM, order.index(name) + 1 - len(LOWPASS_AT) + 4)

        first = Step(None, 0, 2)

        def use0(name):
            return {"q0": 1, "q1": 2, "k0": 3, "k1": 4}[name]

        def final_use(name):
            return NG * NM - len(LOWPASS_AT) + 4 - 4 + sorted(LOWPASS_AT.values(), key=order.index).index(name) + 1

        def use_in(g, name):
            if g.reg is None and g.c == NG - 1 and order.index(name) > order.index("q0"):
                gone = sum(1 for m in ("q0", "q1", "k0", "k1") if order.index(m) < order.index(name))
                return use(g, name) - gone
            return use(g, name)

        def halves(name):
            return int(name[-1])

        def group_steps(eng, body):
            steps(eng, NG - 2, 2, 2, NG, body)

        def batch(eng, g):
            if g.reg is None:
                return g.c // G
            return eng.snap(g.times(1)) // G

        def column(eng, g):
            if g.reg is None:
                return (g.c % G) * P
            return (eng.snap(g.times(1)) % G) * P

        @block.sync
        def _(sp):
            for dst, src in ((cos, "c_cos"), (sin, "c_sin"), (near, "c_near"), (far, "c_far"), (identb, "c_identb"),
                             (mask_s, "c_mask_s"), (mask_t, "c_mask_t"), (headsum, "c_heads")):
                sp.dma_start(dst[:], a[src]).then_inc(s_const, 16)
            for n, name in enumerate(("lambda_q1", "lambda_k1", "lambda_q2", "lambda_k2")):
                sp.dma_start(lam_in[:, n], a[name].rearrange("(o d) -> o d", o=1).broadcast_to([P, D]))\
                    .then_inc(s_const, 16)

            def load_w(g):
                col = column(sp, g)
                for n, name in enumerate(("Wq", "Wk")):
                    sp.dma_start(wg[:, g.slot, :, n],
                                 a[name].rearrange("(c p) n -> p c n", p=P)[:, :, bass.ds(col, P)])\
                        .then_inc(s_wg[g.slot], 16)
                b8 = batch(sp, g) * TB
                sp.dma_start(vg[:, g.slot], v_scr[bass.ds(b8, TB), :, bass.ds(col, P)].rearrange("s p e -> p s e"))\
                    .then_inc(s_vg[g.slot], 16)

            def pieces_out(g, w):
                wait_alone(sp, s_pc, g.times(2, 1 + w), mark_sp)
                if g.past(2):
                    wait_alone(sp, s_stack[w][g.slot], g.round(96), mark_sp)
                sp.dma_start(piece_scr[g.slot, w].rearrange("p r t -> r p t"), pieces[:, w]).then_inc(s_piece[w], 16)

            def stack(g, w):
                wait_alone(sp, s_piece[w], g.times(16, 16), mark_sp)
                if g.past(2):
                    wait_alone(sp, s_pv, g.times(NV, -NV), mark_sp)
                for n, piece in enumerate(((0, 1, 2, 0, 1, 0), (0, 0, 0, 1, 1, 2))[w]):
                    sp.dma_start((qst, kst)[w][n * D:(n + 1) * D, g.slot],
                                 piece_scr[g.slot, w, piece].rearrange("(a d) t -> d a t", d=D))\
                        .then_inc(s_stack[w][g.slot], 16)

            def shift_in(g, h):
                wait_alone(sp, s_shrow, g.times(2, h + 1), mark_sp)
                sp.dma_start(shift_scr[h].rearrange("n a t -> (n a) t"), shrow[:, h]).then_inc(s_shout[h], 16)
                wait_alone(sp, s_shout[h], g.times(16, 16), mark_sp)
                sp.dma_start(qst[PIECES:ROWS, g.slot, :, h * HALF:(h + 1) * HALF], shift_scr[h])\
                    .then_inc(s_shdma[h], 16)

            load_w(first)
            for w in range(2):
                pieces_out(first, w)
                stack(first, w)

            def body(g):
                more = g.reg is not None or g.c < NG - 1
                nxt = g.back(-1)
                if more:
                    if g.past(1):
                        wait_alone(sp, s_pv, g.times(NV), mark_sp)
                        wait_alone(sp, s_mread, use_in(g.back(1), "k1"), mark_sp)
                    load_w(nxt)
                if g.past(1):
                    store(g.back(1))
                shift_in(g, 0)
                if more:
                    pieces_out(nxt, 0)
                    stack(nxt, 0)
                shift_in(g, 1)
                if more:
                    pieces_out(nxt, 1)
                    stack(nxt, 1)

            def store(g):
                wait_alone(sp, s_att, g.times(2, 2), mark_sp)
                sp.dma_start(att_scr[bass.ds(g.times(1), 1)].rearrange("g p t -> p (g t)"), y[:]).then_inc(s_attdma, 16)

            group_steps(sp, body)
            store(Step(None, NG - 1, 2))
            sp.wait_ge(s_attdma, 16 * NG)

        @block.tensor
        def _(pe):
            pe.wait_ge(s_const, 16 * 12)

            def take(number):
                if isinstance(number, int) and number < 2:
                    return
                pe.wait_ge(s_mread, number - 1)

            def project(g, name, number):
                h, w = halves(name), int(name[0] == "k")
                pe.wait_ge(s_wg[g.slot], g.round(32, 32))
                take(number)
                base = batch(pe, g) * T + h * HALF
                for c in range(KC):
                    mm = nc.tensor.matmul(misc[:], wg[:, g.slot, c, w], xnT[:, c, bass.ds(base, HALF)],
                                          start=(c == 0), stop=(c == KC - 1))
                mm.then_inc(s_misc, 1)

            def lowpass(g, name, number):
                h = halves(name)
                take(number)
                if name[0] == "t":
                    pe.wait_ge(s_oT, g.times(2, 2))
                    for i in range(4):
                        j = 4 * h + i
                        mm = nc.tensor.transpose(misc[:, i * P:(i + 1) * P], oT[:, j * P:(j + 1) * P], ident[:])
                elif name[0] == "l":
                    pe.wait_ge(s_nat, g.times(4, 4))
                    for j in range(TB):
                        off = (h * HALF - j * P) % T
                        nc.tensor.matmul(misc[:], onb[:, j], far[:, off:off + HALF], start=(j == 0), stop=(j == TB - 1),
                                         skip_group_check=True)
                    win = near_windows(h)
                    for n, (j, col, t0, cnt) in enumerate(win):
                        mm = nc.tensor.matmul(misc[:, t0:t0 + cnt], onat[:, j], near[:, col:col + cnt], start=False,
                                              stop=True, skip_group_check=True)
                else:
                    pe.wait_ge(s_sq, g.times(2, h + 1))
                    mm = nc.tensor.matmul(misc[:], headsum[:], sq[:, h * HALF:(h + 1) * HALF], start=True, stop=True)
                mm.then_inc(s_misc, 1)

            def shifts(g, name, number):
                h = halves(name)
                take(number)
                pe.wait_ge(s_sh, g.times(2, h + 1))
                for i in range(SH):
                    mm = nc.tensor.transpose(miscb[0:3 * NP, i * P:(i + 1) * P],
                                             shp[:, h * SH + i].rearrange("p a b -> p (a b)"), identb[:])
                mm.then_inc(s_misc, 1)

            def slot_free(g, n):
                if n >= NSLOT:
                    pe.wait_ge(s_exp, g.times(UN, n - NSLOT + 1))
                elif g.past(1):
                    before = max(m for m in range(UN) if m % NSLOT == n)
                    pe.wait_ge(s_exp, g.times(UN, before + 1 - UN))

            def rows(g, n):
                i, pair, cnt = RU[n]
                slot = (n) % NSLOT
                slot_free(g, n)
                width = (i + 1) * P
                for k in range(cnt):
                    for c0 in range(0, width, HALF):
                        w = min(HALF, width - c0)
                        bank = k if cnt == 2 else c0 // HALF
                        diag = c0 + w == width
                        mm = nc.tensor.matmul(score[slot][:, bank, 0:w],
                                              qst[0:PIECES, g.slot, pair + k, i * P:(i + 1) * P],
                                              kst[0:PIECES, g.slot, pair + k, c0:c0 + w], start=True, stop=True)
                        if diag:
                            mm = nc.tensor.matmul(score[slot][:, bank, w - P:w], identb[:], mask_s[:],
                                                  start=False, stop=True, skip_group_check=True)
                mm.then_inc(s_slot, 1)

            def probs(g, m):
                h, j, which, head = PU[m]
                n = NU + m
                slot = n % NSLOT
                slot_free(g, n)
                t0 = max(j * P - h * HALF, 0)
                for k in range(2):
                    pair = 2 * (head + k) + which
                    diag = j >= 4 * h
                    mm = nc.tensor.matmul(score[slot][:, k, t0:HALF], kst[0:ROWS, g.slot, pair, j * P:(j + 1) * P],
                                          qst[0:ROWS, g.slot, pair, h * HALF + t0:(h + 1) * HALF],
                                          start=True, stop=True)
                    if diag:
                        mm = nc.tensor.matmul(score[slot][:, k, t0:t0 + P], identb[:], mask_t[:],
                                              start=False, stop=True, skip_group_check=True)
                mm.then_inc(s_slot, 1)

            def values(g, m):
                h, j, which, _ = PU[m]
                pe.wait_ge(s_exp, g.times(UN, NU + m + 1))
                t0 = max(j * P - h * HALF, 0)
                if j == 0 and which == 0:
                    if g.reg is not None or g.c > 0 or h:
                        pe.wait_ge(s_oT, g.times(2, h))
                end = j == (h + 1) * TB // 2 - 1 and which == 1
                for head in range(GH):
                    pslot = (m - 1 + head // 2) % NPROB
                    v = (vg, vn)[which]
                    mm = nc.tensor.matmul(acc[head * 32:head * 32 + 32, t0:HALF],
                                          v[:, g.slot, j, head * 32:head * 32 + 32],
                                          prob[:, pslot, head % 2, t0:HALF],
                                          start=(j == 0 and which == 0), stop=end, skip_group_check=True)
                mm.then_inc(s_pv, 1)

            def last_lowpass(g):
                for name in [LOWPASS_AT[n] for n in sorted(LOWPASS_AT)]:
                    lowpass(g, name, final_use(name))

            for name in ("q0", "q1", "k0", "k1"):
                project(first, name, use0(name))

            def body(g):
                for w in range(2):
                    pe.wait_ge(s_stack[w][g.slot], g.round(96, 96))
                for n in range(NU):
                    rows(g, n)
                    if n in LOWPASS_AT and g.past(1):
                        lowpass(g.back(1), LOWPASS_AT[n], use_in(g, LOWPASS_AT[n]))
                    if n in PROJECT_AT and (g.reg is not None or g.c < NG - 1):
                        project(g.back(-1), PROJECT_AT[n], use_in(g, PROJECT_AT[n]))
                    if n == SHIFT0_AT:
                        shifts(g, "shift0", use_in(g, "shift0"))
                pe.wait_ge(s_vg[g.slot], g.round(16, 16))
                pe.wait_ge(s_vn, g.times(1, 1))
                pe.wait_ge(s_ones, 1)
                for m in range(NQ):
                    if m == 0:
                        pe.wait_ge(s_shdma[0], g.times(16, 16))
                    if PU[m][0] == 1 and PU[m - 1][0] == 0:
                        pe.wait_ge(s_shdma[1], g.times(16, 16))
                    probs(g, m)
                    if m == SHIFT1_AT:
                        shifts(g, "shift1", use_in(g, "shift1"))
                    if m >= 3 and m % 2:
                        values(g, m - 2)
                values(g, NQ - 1)
            group_steps(pe, body)
            last_lowpass(Step(None, NG - 1, 2))

        @block.vector
        def _(dve):
            dve.wait_ge(s_const, 16 * 12)
            nc.vector.tensor_tensor(lam_p[:, 0], lam_in[:, 0], lam_in[:, 1], ALU.mult).then_inc(s_lam, 1)
            nc.vector.tensor_tensor(lam_p[:, 1], lam_in[:, 2], lam_in[:, 3], ALU.mult).then_inc(s_lam, 1)
            dve.wait_ge(s_lam, 2)
            nc.vector.tensor_reduce(lam_e[:], lam_p[:], AX.X, ALU.add).then_inc(s_lam, 1)
            dve.wait_ge(s_lam, 4)
            nc.vector.tensor_tensor(nlam[:], lam_e[:, 1], lam_e[:, 0], ALU.subtract).then_inc(s_lam, 1)
            dve.wait_ge(s_lam, 5)
            nc.vector.tensor_scalar(nlam[:], nlam[:], LAMBDA_INIT, None, ALU.subtract).then_inc(s_lam, 1)

            def project(g, name, number):
                h, w = halves(name), int(name[0] == "k")
                cols = slice(h * HALF, (h + 1) * HALF)
                dve.wait_ge(s_misc, number)
                if g.past(1):
                    dve.wait_ge(s_cosm, g.times(2, w - 1))
                nc.vector.tensor_scalar(raw[:, w, cols], misc[:], (1.0, float(D) ** -0.5)[w], None, ALU.mult)\
                    .then_inc(s_mread, 1)
                if h == 1:
                    wait_alone(dve, s_mread, number, mark_dve)
                    if g.past(1):
                        wait_alone(dve, s_pc, g.times(2, w - 1), mark_dve)
                    nc.vector.stream_shuffle(swapped[:, w], raw[:, w], [i ^ 1 for i in range(32)])\
                        .then_inc(s_swap, 1)

            def lowpass(g, name, number):
                h = halves(name)
                cols = slice(h * HALF, (h + 1) * HALF)
                dve.wait_ge(s_misc, number)
                if name[0] == "t":
                    dst, dstb = onat[:, 4 * h:4 * h + 4], onb[:, 4 * h:4 * h + 4]
                    src = misc[:].rearrange("p (j c) -> p j c", j=4)
                    nc.vector.tensor_copy(dst, src).then_inc(s_nat, 1)
                    nc.vector.tensor_copy(dstb, src).then_inc(s_nat, 1)
                    dve.wait_ge(s_nat, g.times(4, 2 * h + 2))
                    dve.sem_inc(s_mread, 1)
                elif name[0] == "l":
                    if g.past(1):
                        dve.wait_ge(s_attdma, g.times(16))
                    nc.vector.tensor_copy(y[:, cols], misc[:]).then_inc(s_y, 1)
                    dve.wait_ge(s_y, g.times(2, h + 1))
                    dve.sem_inc(s_mread, 1)
                else:
                    dve.wait_ge(s_sq, g.times(2, h + 1))
                    nc.vector.tensor_scalar(sq[:, cols], misc[:], EPS, None, ALU.add).then_inc(s_mread, 1)

            def shift_pieces(g, h):
                c = slice(h * SH, (h + 1) * SH)
                ch = Chain(dve, s_chain, g, 10)
                ch.n = 5 * h
                dve.wait_ge(s_ln, g.times(2, h + 1))
                ch.link(nc.vector.tensor_tensor(shift[:, :, c], nmax[:, :, c], den[:, :, c], ALU.subtract))
                out = shp[:, c].rearrange("p i n a -> p n a i")
                ch.link(nc.vector.tensor_copy(out[:, 0], shift[:, :, c]))
                ch.link(nc.vector.tensor_tensor(rest[:, :, c], shift[:, :, c], out[:, 0], ALU.subtract))
                ch.link(nc.vector.tensor_copy(out[:, 1], rest[:, :, c]))
                ch.n += 1
                nc.vector.tensor_tensor(out[:, 2], rest[:, :, c], out[:, 1], ALU.subtract).then_inc(s_chain, 1)
                dve.wait_ge(s_chain, g.times(10, ch.n))
                dve.sem_inc(s_sh, 1)

            def shift_rows(g, name, number):
                h = halves(name)
                dve.wait_ge(s_misc, number)
                if g.past(1):
                    dve.wait_ge(s_shout[h], g.times(16))
                nc.vector.tensor_copy(shrow[:, h], miscb[0:3 * NP, 0:HALF]).then_inc(s_shrow, 1)
                dve.wait_ge(s_shrow, g.times(2, h + 1))
                dve.sem_inc(s_mread, 1)

            for name in ("q0", "q1", "k0", "k1"):
                project(first, name, use0(name))

            def body(g):
                for n in range(NU):
                    i, pair, cnt = RU[n]
                    dve.wait_ge(s_slot, g.times(UN, n + 1))
                    if n == 0 and g.past(1):
                        dve.wait_ge(s_exp, g.times(UN, NU - UN))
                    src = score[n % NSLOT]
                    if cnt == 2:
                        nc.vector.tensor_reduce(nmax[:, pair:pair + 2, i:i + 1], src[:, :, 0:(i + 1) * P], AX.X,
                                                ALU.max, negate=True).then_inc(s_max, 1)
                    else:
                        nc.vector.tensor_reduce(nmax[:, pair, i:i + 1],
                                                src[:].rearrange("p a b -> p (a b)")[:, 0:(i + 1) * P], AX.X,
                                                ALU.max, negate=True).then_inc(s_max, 1)
                    m = n - 1
                    if m in LOWPASS_AT and g.past(1):
                        lowpass(g.back(1), LOWPASS_AT[m], use_in(g, LOWPASS_AT[m]))
                    if m in PROJECT_AT and (g.reg is not None or g.c < NG - 1):
                        project(g.back(-1), PROJECT_AT[m], use_in(g, PROJECT_AT[m]))
                    if n == 22:
                        shift_pieces(g, 0)
                    if m == SHIFT0_AT:
                        shift_rows(g, "shift0", use_in(g, "shift0"))
                shift_pieces(g, 1)
                shift_rows(g, "shift1", use_in(g, "shift1"))
                for h in range(2):
                    dve.wait_ge(s_pv, g.times(NV, (NV // 3, NV)[h]))
                    nc.vector.tensor_copy(oT[:, h * HALF:(h + 1) * HALF], acc[:]).then_inc(s_oT, 1)
            group_steps(dve, body)
            g = Step(None, NG - 1, 2)
            for n in sorted(LOWPASS_AT):
                lowpass(g, LOWPASS_AT[n], final_use(LOWPASS_AT[n]))

        @block.scalar
        def _(act):
            nc.scalar.preload_act_table_set("natural_log_exp_and_others")
            act.wait_ge(s_lam, 3)
            nc.scalar.activation(lam_e[:], lam_e[:], ACT.Exp).then_inc(s_lam, 1)

            def log(g, h):
                c = slice(h * SH, (h + 1) * SH)
                upto = max(n for n, u in enumerate(RU) if u[0] < SH * (h + 1)) + 1
                act.wait_ge(s_exp, g.times(UN, upto))
                nc.scalar.activation(den[:, :, c], den[:, :, c], ACT.Ln).then_inc(s_ln, 1)

            def root(g, h, number):
                act.wait_ge(s_mread, number)
                if h or g.past(1):
                    act.wait_ge(s_newton, g.times(8, 4 * h))
                nc.scalar.activation(rs[:], sq[:, h * HALF:(h + 1) * HALF], ACT.Ln).then_inc(s_rs, 1)
                act.wait_ge(s_rs, g.times(4, 2 * h + 1))
                nc.scalar.activation(rs[:], rs[:], ACT.Exp, scale=-0.5).then_inc(s_rs, 1)

            def body(g):
                for n in range(NU):
                    i, pair, cnt = RU[n]
                    if n in ROOT_AT and g.past(1):
                        h = ROOT_AT[n]
                        root(g.back(1), h, use_in(g, f"square{h}"))
                    if n == 0 and g.past(1):
                        act.wait_ge(s_chain, g.times(10))
                    act.wait_ge(s_max, g.times(NU, n + 1))
                    src = score[n % NSLOT]
                    for k in range(cnt):
                        s = src[:, k, 0:(i + 1) * P] if cnt == 2 else \
                            src[:].rearrange("p a b -> p (a b)")[:, 0:(i + 1) * P]
                        ins = nc.scalar.activation(s, s, ACT.Exp, bias=nmax[:, pair + k, i:i + 1],
                                                   accum_out=den[:, pair + k, i:i + 1])
                    ins.then_inc(s_exp, 1)
                    if n == 18:
                        log(g, 0)
                log(g, 1)
                for m in range(NQ):
                    h, j, which, head = PU[m]
                    act.wait_ge(s_slot, g.times(UN, NU + m + 1))
                    if g.reg is not None or g.c * NQ + m >= NPROB:
                        act.wait_ge(s_pv, g.times(NV, (m - NPROB) // 2 + 1))
                    t0 = max(j * P - h * HALF, 0)
                    nc.scalar.activation(prob[:, m % NPROB, :, t0:HALF], score[(NU + m) % NSLOT][:, :, t0:HALF],
                                         ACT.Exp).then_inc(s_exp, 1)
            group_steps(act, body)
            for h in range(2):
                root(Step(None, NG - 1, 2), h, final_use(f"square{h}"))

        @block.gpsimd
        def _(pool):
            pool.wait_ge(s_const, 16 * 12)
            nc.gpsimd.memset(kst[PIECES:ROWS + 29, 0:2], 1.0).then_inc(s_ones, 1)
            pool.wait_ge(s_ones, 1)

            def scale_v(g):
                wait_alone(pool, s_vg[g.slot], g.round(16, 16), mark_pool)
                if not g.past(1):
                    pool.wait_ge(s_lam, 6)
                if g.past(2):
                    wait_alone(pool, s_pv, g.times(NV, -NV), mark_pool)
                nc.gpsimd.tensor_scalar(vn[:, g.slot], vg[:, g.slot], nlam[:], None, ALU.mult).then_inc(s_vn, 1)

            def rotate(g, w):
                ch = Chain(pool, s_rot, g, 12, mark_pool)
                ch.n = 6 * w
                wait_alone(pool, s_swap, g.times(2, w + 1), mark_pool)
                nc.gpsimd.tensor_tensor(rot[:], raw[:, w], cos[:], ALU.mult).then_inc(s_cosm, 1)
                ch.link(nc.gpsimd.tensor_tensor(swapped[:, w], swapped[:, w], sin[:], ALU.mult))
                wait_alone(pool, s_cosm, g.times(2, w + 1), mark_pool)
                ch.link(nc.gpsimd.tensor_tensor(rot[:], rot[:], swapped[:, w], ALU.add))
                if g.past(1):
                    wait_alone(pool, s_piece[w], g.times(16), mark_pool)
                ch.link(nc.gpsimd.tensor_copy(pieces[:, w, 0], rot[:]))
                ch.link(nc.gpsimd.tensor_tensor(rot[:], rot[:], pieces[:, w, 0], ALU.subtract))
                ch.link(nc.gpsimd.tensor_copy(pieces[:, w, 1], rot[:]))
                ch.link(nc.gpsimd.tensor_tensor(pieces[:, w, 2], rot[:], pieces[:, w, 1], ALU.subtract))
                pool.sem_inc(s_pc, 1)

            def squares(g, h):
                cols = slice(h * HALF, (h + 1) * HALF)
                wait_alone(pool, s_y, g.times(2, h + 1), mark_pool)
                if g.past(1):
                    wait_alone(pool, s_att, g.times(2, h - 1), mark_pool)
                nc.gpsimd.tensor_tensor(sq[:, cols], y[:, cols], y[:, cols], ALU.mult).then_inc(s_sq, 1)

            def normalised(g, h):
                cols = slice(h * HALF, (h + 1) * HALF)
                ch = Chain(pool, s_newton, g, 8, mark_pool)
                ch.n = 4 * h
                wait_alone(pool, s_rs, g.times(4, 2 * h + 2), mark_pool)
                ch.link(nc.gpsimd.tensor_tensor(newton[:], rs[:], rs[:], ALU.mult))
                ch.link(nc.gpsimd.tensor_tensor(newton[:], newton[:], sq[:, cols], ALU.mult))
                ch.link(nc.gpsimd.tensor_scalar(newton[:], newton[:], -0.5, 1.5, ALU.mult, ALU.add))
                ch.link(nc.gpsimd.tensor_tensor(newton[:], newton[:], rs[:], ALU.mult))
                nc.gpsimd.tensor_tensor(y[:, cols], y[:, cols], newton[:], ALU.mult).then_inc(s_att, 1)
                wait_alone(pool, s_att, g.times(2, h + 1), mark_pool)

            scale_v(first)
            for w in range(2):
                rotate(first, w)

            def body(g):
                if g.past(1):
                    for h in range(2):
                        squares(g.back(1), h)
                    for h in range(2):
                        normalised(g.back(1), h)
                if g.reg is not None or g.c < NG - 1:
                    for w in range(2):
                        rotate(g.back(-1), w)
                    scale_v(g.back(-1))
            group_steps(pool, body)
            g = Step(None, NG - 1, 2)
            for h in range(2):
                squares(g, h)
            for h in range(2):
                normalised(g, h)




R = 4
NH = NX * IX
NHL = NH + NX


class Experts:

    def __init__(self, nc, ctx, pre, w, mark_pool, mark_dve):
        def sb(name, shape, dt=F32):
            return ctx.enter_context(nc.sbuf_tensor(pre + name, shape, dt))

        def sem(name):
            return ctx.enter_context(nc.semaphore(pre + name))
        self.mark_pool, self.mark_dve = mark_pool, mark_dve
        self.nc, self.w = nc, w
        self.x, self.n1, self.x2 = sb("x", [P, R, E]), sb("n1", [P, 2, E]), sb("x2", [P, R, E])
        self.n1T = sb("n1T", [P, 2, E])
        self.st, self.mv, self.rstd = sb("st", [P, R, 6]), sb("mv", [P, R, 2]), sb("rstd", [P, R, 1])
        self.half = sb("half", [P, 1])
        self.e, self.top, self.we = sb("e", [P, 2, NH]), sb("top", [P, 2, 1]), sb("we", [P, 2, NX])
        self.tot = sb("tot", [P, 2, 1])
        self.gt, self.eq = sb("gt", [P, NX, NX]), sb("eq", [P, NX, NX])
        self.rank, self.gate = sb("rank", [P, NX]), sb("gate", [P, NX])
        self.ga, self.gaT = sb("ga", [P, 2, NH]), sb("gaT", [P, 2, P])
        self.s_x, self.s_stat, self.s_var, self.s_rstd = sem("s_x"), sem("s_stat"), sem("s_var"), sem("s_rstd")
        self.s_half, self.s_n1, self.s_t1, self.s_n1T = sem("s_half"), sem("s_n1"), sem("s_t1"), sem("s_n1T")
        self.s_h, self.s_top, self.s_e, self.s_gate = sem("s_h"), sem("s_top"), sem("s_e"), sem("s_gate")
        self.s_ga, self.s_tg, self.s_gaT, self.s_u, self.s_x2 = (sem(n) for n in ("s_ga", "s_tg", "s_gaT", "s_u",
                                                                                 "s_x2"))

    def dve_stats(self, dve, t):
        dve.wait_ge(self.s_x, t.times(1, 1))
        self.nc.vector.bn_stats(self.st[:, t.slot], self.x[:, t.slot]).then_inc(self.s_stat, 1)
        wait_alone(dve, self.s_stat, t.times(2, 1), self.mark_dve)
        self.nc.vector.bn_aggr(self.mv[:, t.slot], self.st[:, t.slot]).then_inc(self.s_stat, 1)

    def dve_norm(self, dve, t):
        dve.wait_ge(self.s_rstd, t.times(1, 1))
        if t.past(2):
            dve.wait_ge(self.s_t1, t.times(1, -1))
        self.nc.vector.tensor_scalar(self.n1[:, t.c % 2], self.x[:, t.slot], self.mv[:, t.slot, 0:1],
                                     self.rstd[:, t.slot], ALU.subtract, ALU.mult).then_inc(self.s_n1, 1)

    def dve_top(self, dve, t, hl):
        dve.wait_ge(self.s_h, t.times(1, 1))
        if t.past(2):
            dve.wait_ge(self.s_e, t.times(2, -2))
        self.nc.vector.tensor_reduce(self.top[:, t.c % 2], hl[:, NH:NHL], AX.X, ALU.max, negate=True)\
            .then_inc(self.s_top, 1)

    def dve_gate(self, dve, t, hl):
        v, k = self.nc.vector, t.c % 2
        ch = Chain(dve, self.s_gate, t, 11)
        dve.wait_ge(self.s_e, t.times(2, 2))
        we = self.we[:, k]
        other = we.rearrange("p (o e) -> p o e", o=1).broadcast_to([P, NX, NX])
        own = we.rearrange("p (e o) -> p e o", o=1).broadcast_to([P, NX, NX])
        ch.link(v.tensor_tensor(self.eq[:], other, own, ALU.is_equal))
        ch.link(v.tensor_tensor(self.gt[:], other, own, ALU.is_gt))
        ch.link(v.tensor_tensor(self.eq[:], self.eq[:], self.w["tri"][:], ALU.mult))
        ch.link(v.tensor_tensor(self.gt[:], self.gt[:], self.eq[:], ALU.add))
        ch.link(v.tensor_reduce(self.rank[:], self.gt[:], AX.X, ALU.add))
        ch.link(v.scalar_tensor_tensor(self.gate[:], self.rank[:], 1.5, we, ALU.is_lt, ALU.mult))
        ch.link(v.reciprocal(self.tot[:, k], self.tot[:, k]))
        ch.link(v.tensor_scalar(self.gate[:], self.gate[:], self.tot[:, k], None, ALU.mult))
        ch.link(v.tensor_scalar(self.e[:, k], self.e[:, k], 1.0, None, ALU.add))
        ch.link(v.reciprocal(self.e[:, k], self.e[:, k]))
        ch.link(v.tensor_tensor(self.e[:, k], self.e[:, k], hl[:, 0:NH], ALU.mult))
        ch.end()
        if t.past(2):
            dve.wait_ge(self.s_tg, t.times(1, -1))
        v.tensor_tensor(self.ga[:, k].rearrange("p (e i) -> p e i", e=NX),
                        self.e[:, k].rearrange("p (e i) -> p e i", e=NX),
                        self.gate[:].rearrange("p (e o) -> p e o", o=1).broadcast_to([P, NX, IX]), ALU.mult)\
            .then_inc(self.s_ga, 1)
        dve.wait_ge(self.s_ga, t.times(1, 1))

    def dve_sum(self, dve, t, bank):
        dve.wait_ge(self.s_u, t.times(1, 1))
        self.nc.vector.tensor_tensor(self.x2[:, t.slot], bank[:], self.x[:, t.slot], ALU.add).then_inc(self.s_x2, 1)

    def pool_start(self, pool):
        self.nc.gpsimd.memset(self.half[:], -0.5).then_inc(self.s_half, 1)
        pool.wait_ge(self.s_half, 1)

    def pool_rstd(self, pool, t):
        g = self.nc.gpsimd
        wait_alone(pool, self.s_stat, t.times(2, 2), self.mark_pool)
        if t.past(R):
            wait_alone(pool, self.s_n1, t.times(1, 1 - R), self.mark_pool)
        g.tensor_scalar(self.rstd[:, t.slot], self.mv[:, t.slot, 1:2], EPS, None, ALU.add).then_inc(self.s_var, 1)
        wait_alone(pool, self.s_var, t.times(1, 1), self.mark_pool)
        g.tensor_tensor(self.rstd[:, t.slot], self.rstd[:, t.slot], self.half[:], ALU.pow).then_inc(self.s_rstd, 1)

    def act_n1T(self, act, t, bank):
        act.wait_ge(self.s_t1, t.times(1, 1))
        if t.past(2):
            act.wait_ge(self.s_h, t.times(1, -1))
        self.nc.scalar.copy(self.n1T[:, t.c % 2], bank[:]).then_inc(self.s_n1T, 1)

    def act_exps(self, act, t, hl):
        k = t.c % 2
        act.wait_ge(self.s_top, t.times(1, 1))
        if t.past(2):
            act.wait_ge(self.s_ga, t.times(1, -1))
        self.nc.scalar.activation(self.e[:, k], hl[:, 0:NH], ACT.Exp, scale=-1.0).then_inc(self.s_e, 1)
        self.nc.scalar.activation(self.we[:, k], hl[:, NH:NHL], ACT.Exp, bias=self.top[:, k],
                                  accum_out=self.tot[:, k]).then_inc(self.s_e, 1)

    def act_gaT(self, act, t, bank):
        act.wait_ge(self.s_tg, t.times(1, 1))
        if t.past(2):
            act.wait_ge(self.s_u, t.times(1, -1))
        self.nc.scalar.copy(self.gaT[:, t.c % 2], bank[:, 0:P]).then_inc(self.s_gaT, 1)

    def pe_turn(self, pe, t, bank):
        pe.wait_ge(self.s_n1, t.times(1, 1))
        for c in range(KC):
            mm = self.nc.tensor.transpose(bank[:, c * P:(c + 1) * P], self.n1[:, t.c % 2, c * P:(c + 1) * P],
                                          self.w["ident"][:])
        mm.then_inc(self.s_t1, 1)

    def pe_down(self, pe, t, hl):
        pe.wait_ge(self.s_n1T, t.times(1, 1))
        if t.past(1):
            pe.wait_ge(self.s_ga, t.times(1))
        for c in range(KC):
            mm = self.nc.tensor.matmul(hl[:, 0:NHL], self.n1T[:, t.c % 2, c * P:(c + 1) * P], self.w["down"][:, c],
                                       start=(c == 0), stop=(c == KC - 1))
        mm.then_inc(self.s_h, 1)

    def pe_turn_ga(self, pe, t, bank):
        pe.wait_ge(self.s_ga, t.times(1, 1))
        self.nc.tensor.transpose(bank[:, 0:P], self.ga[:, t.c % 2], self.w["ident"][:]).then_inc(self.s_tg, 1)

    def pe_up(self, pe, t, bank):
        pe.wait_ge(self.s_gaT, t.times(1, 1))
        if t.past(1):
            pe.wait_ge(self.s_x2, t.times(1))
        self.nc.tensor.matmul(bank[:], self.gaT[:, t.c % 2], self.w["up"][:], start=True, stop=True)\
            .then_inc(self.s_u, 1)



def middle(nc, a, x_tiles, att_scr, qt_scr, res_scr, w):
    with ExitStack() as ctx:
        def sb(name, shape, dt=F32):
            return ctx.enter_context(nc.sbuf_tensor("m_" + name, shape, dt))

        def sem(name):
            return ctx.enter_context(nc.semaphore("m_" + name))
        mark_sp, mark_pool, mark_dve = (sem(f"m_mark_{e}") for e in ("sp", "pool", "dve"))

        def bank(name):
            return ctx.enter_context(nc.psum_tensor("m_" + name, [P, E], F32))
        ident, wab, bout = w["ident"], w["wab"], w["bout"]
        ex = Experts(nc, ctx, "m_", w, mark_pool, mark_dve)
        wo = sb("wo", [P, KC, E])
        rms = sb("rms", [P, 1])
        win = sb("win", [P, KC, 3 * E])
        lnw, lnb, ones = sb("lnw", [P, KC]), sb("lnb", [P, KC]), sb("ones", [P, P])
        lnbb = sb("lnbb", [P, KC, P])
        bin_ = sb("bin", [P, 3 * E])
        wout = sb("wout", [P, KC, E])
        which = sb("which", [P, NT, B])
        aT = sb("aT", [P, 2, KC, P])
        xin = sb("xin", [P, 2, E])
        rope = sb("rope", [P, 2, 2, NROPE])
        st2, mv2 = sb("st2", [P, R, 6]), sb("mv2", [P, R, 2])
        r1, v2, r12 = sb("r1", [P, R, 1]), sb("v2", [P, R, 1]), sb("r12", [P, R, 1])
        n2, h2 = sb("n2", [P, 2, E]), sb("h2", [P, 2, E])
        hT = sb("hT", [P, 2, E])
        q, k, v = sb("q", [P, 2, E]), sb("k", [P, 2, E]), sb("v", [P, 2, E])
        sw, sq = sb("sw", [P, NROPE]), sb("sq", [P, E])
        ss, rinv = sb("ss", [P, 2, 1]), sb("rinv", [P, 2, 1])
        wr = sb("wr", [P, 2, B])
        qT = sb("qT", [P, 2, KC, P])
        arow = sb("arow", [B, E])
        acol = sb("acol", [P, KC, B])

        t0, t1, hl, bw, bu, b0, b1, ba = (bank(n) for n in ("t0", "t1", "hl", "bw", "bu", "b0", "b1", "ba"))
        s_const, s_constb, s_prep, s_bias, s_fold = (sem(n) for n in ("const", "constb", "prep", "bias", "fold"))
        s_in = [sem(f"in{i}") for i in range(2)]
        s_w, s_st2, s_rr, s_n2, s_h2 = sem("w"), sem("st2"), sem("rr"), sem("n2"), sem("h2")
        s_t2, s_hT, s_q, s_k, s_v, s_kb, s_vb, s_qb = (sem(n) for n in ("t2", "hT", "q", "k", "v", "kb", "vb", "qb"))
        s_ss, s_rope, s_kv, s_qr, s_wr, s_acc, s_tq, s_qT = (sem(n) for n in ("ss", "rope", "kv", "qr", "wr", "acc",
                                                                             "tq", "qT"))
        s_res, s_tail, s_fold2, s_ropein, s_wrc, s_rrc = (sem(n) for n in ("res", "tail", "fold2", "ropein", "wrc",
                                                                          "rrc"))
        res = sb("res", [P, R, E])
        s_resd = [sem(f"resd{i}") for i in range(R)]
        s_qTd = [sem(f"qTd{i}") for i in range(2)]
        NCONST, NCONSTB = 6 + GH, 6 + KC
        block = ctx.enter_context(nc.Block())

        def modulo(eng, t):
            return t.c % TB if t.reg is None else eng.snap(t.times(1)) % TB

        def batch(eng, t):
            return t.c // TB if t.reg is None else eng.snap(t.times(1)) // TB

        def by2(t, per, add=0):
            if t.reg is None:
                return (t.c // 2) * per + add
            return t.reg * (t.stride // 2 * per) + ((t.c // 2) * per + add)

        @block.sync
        def _(sp):
            def load_tile(t):
                if t.past(2):
                    wait_alone(sp, ex.s_x, t.times(1, -1), mark_sp)
                time = modulo(sp, t)
                b4 = batch(sp, t) * G
                k_ = t.c % 2
                sp.dma_start(aT[:, k_], att_scr[bass.ds(b4, G), :, bass.ds(time * P, P)]
                             .rearrange("g p t -> p g t")).then_inc(s_in[k_], 16)
                sp.dma_start(xin[:, k_], x_tiles[bass.ds(t.times(1), 1)].rearrange("a p e -> p (a e)"))\
                    .then_inc(s_in[k_], 16)

            consts = [(wo[:], a["Wout"].rearrange("(c p) n -> p c n", p=P)),
                      (ident[:], a["c_ident"]),
                      (w["down"][:, :, 0:NH], a["down_w"].rearrange("(c p) e i -> p c (e i)", p=P)),
                      (w["down"][:, :, NH:NHL], a["router_w"].rearrange("(c p) e -> p c e", p=P)),
                      (w["tri"][:], a["c_tri"].rearrange("p (e f) -> p e f", e=NX)),
                      (w["up"][:], a["up_w"].rearrange("e i h -> (e i) h"))]
            consts += [(rms[n * 2 * D:(n + 1) * 2 * D], a["rms_weight"].rearrange("(p o) -> p o", o=1))
                       for n in range(GH)]
            later = [(bout[:], a["b_out"].rearrange("(o n) -> o n", o=1).broadcast_to([P, E])),
                     (which[:], a["c_which"].rearrange("p (t b) -> p t b", b=B)),
                     (lnw[:], a["ln_w"].rearrange("(c p) -> p c", p=P)),
                     (lnb[:], a["ln_b"].rearrange("(c p) -> p c", p=P)),
                     (bin_[:], a["b_in"].rearrange("(o n) -> o n", o=1).broadcast_to([P, 3 * E]))]
            later += [(win[:, c], a["W_in"].rearrange("(c p) n -> c p n", p=P)[c]) for c in range(KC)]
            later += [(wout[:], a["W_out"].rearrange("(c p) n -> p c n", p=P))]
            assert (len(consts), len(later)) == (NCONST, NCONSTB)
            for dst, src in consts:
                sp.dma_start(dst, src, allow_slow_non_contiguous=True).then_inc(s_const, 16)
            load_tile(Step(None, 0, R))
            load_tile(Step(None, 1, R))
            for dst, src in later:
                sp.dma_start(dst, src, allow_slow_non_contiguous=True).then_inc(s_constb, 16)

            def body(t):
                if t.reg is not None or t.c >= 2:
                    load_tile(t)
            steps(sp, NT, R, 2 * R, NT, body)

        @block.tensor
        def _(pe):
            mmul = nc.tensor.matmul
            pe.wait_ge(s_const, 16 * NCONST)
            pe.wait_ge(s_fold, KC)

            def project(t, b, part, done):
                for c in range(KC):
                    mm = mmul(b[:], hT[:, t.c % 2, c * P:(c + 1) * P], win[:, c, part * E:(part + 1) * E],
                              start=(c == 0), stop=(c == KC - 1))
                mm.then_inc(done, 1)

            def body(s):
                t = s
                if t.exists(NT):
                    pe.wait_ge(s_in[t.c % 2], by2(t, 32, 32))
                    if t.past(1):
                        pe.wait_ge(ex.s_x, t.times(1))
                    for c in range(KC):
                        mm = mmul(bw[:], aT[:, t.c % 2, c], wo[:, c], start=(c == 0), stop=(c == KC - 1))
                    mm.then_inc(s_w, 1)
                t = s.back(1)
                if t.exists(NT):
                    if t.past(4):
                        pe.wait_ge(s_qT, t.times(1, -3))
                    ex.pe_turn(pe, t, t0)
                t = s.back(3)
                if t.exists(NT):
                    pe.wait_ge(s_h2, t.times(1, 1))
                    if t.past(1):
                        pe.wait_ge(ex.s_gaT, t.times(1, 1))
                    for c in range(KC):
                        mm = nc.tensor.transpose(t1[:, c * P:(c + 1) * P], h2[:, t.c % 2, c * P:(c + 1) * P], ident[:])
                    mm.then_inc(s_t2, 1)
                t = s.back(2)
                if t.exists(NT):
                    if s.back(3).exists(NT):
                        pe.wait_ge(s_hT, s.back(3).times(1, 1))
                    ex.pe_turn_ga(pe, t, t1)
                t = s.back(1)
                if t.exists(NT):
                    ex.pe_down(pe, t, hl)
                t = s.back(2)
                if t.exists(NT):
                    ex.pe_up(pe, t, bu)
                if s.reg is None and s.c == 2:
                    pe.wait_ge(s_constb, 16 * NCONSTB)
                    pe.wait_ge(s_prep, 1)
                    for n, b in enumerate((b0, b1, ba)):
                        for c in range(KC):
                            mm = mmul(b[:], lnbb[:, c], win[:, c, n * E:(n + 1) * E], start=(c == 0),
                                      stop=(c == KC - 1))
                        mm.then_inc(s_bias, 1)
                if s.reg is None and s.c == 3:
                    pe.wait_ge(s_fold2, 3 + KC)
                t = s.back(3)
                if t.exists(NT):
                    pe.wait_ge(s_hT, t.times(1, 1))
                    for n, (b, done) in enumerate(((b0, s_k), (b1, s_v))):
                        if t.past(1):
                            pe.wait_ge((s_qb, s_vb)[n], t.times(1))
                        project(t, b, 1 + n, done)
                t = s.back(4)
                if t.exists(NT):
                    pe.wait_ge(s_qr, t.times(1, 1))
                    pe.wait_ge(ex.s_n1T, s.back(1).times(1, 1) if s.back(1).exists(NT) else NT)
                    if t.past(1) and not s.back(1).exists(NT):
                        pe.wait_ge(s_qT, t.times(1))
                    for c in range(KC):
                        mm = nc.tensor.transpose(t0[:, c * P:(c + 1) * P], q[:, t.c % 2, c * P:(c + 1) * P], ident[:])
                    mm.then_inc(s_tq, 1)
                t = s.back(4)
                if t.exists(NT):
                    pe.wait_ge(s_kv, t.times(1, 1))
                    pe.wait_ge(s_wr, t.times(1, 1))
                    one = t.reg is None
                    mmul(ba[0:B, :], wr[:, t.c % 2], k[:, t.c % 2], start=(one and t.c == 0),
                         stop=(one and t.c == NT - 1)).then_inc(s_acc, 1)
                t = s.back(3)
                if t.exists(NT):
                    pe.wait_ge(s_kb, t.times(1, 1))
                    project(t, b0, 0, s_q)
            steps(pe, NT, R, 2 * R, NT + 4, body)
            pe.wait_ge(s_tail, 1)
            for c in range(KC):
                mm = nc.tensor.transpose(t1[:, c * B:(c + 1) * B], arow[:, c * P:(c + 1) * P], ident[0:B, 0:B])
            mm.then_inc(s_tail, 1)

        @block.vector
        def _(dve):
            vec = nc.vector
            dve.wait_ge(s_const, 16 * NCONST)
            for c in range(KC):
                vec.tensor_scalar(wo[:, c], wo[:, c], rms[:], 1.0 - LAMBDA_INIT, ALU.mult, ALU.mult)\
                    .then_inc(s_fold, 1)

            def body(s):
                t = s
                if t.exists(NT):
                    dve.wait_ge(s_w, t.times(1, 1))
                    if t.past(R):
                        dve.wait_ge(ex.s_x2, t.times(1, 1 - R))
                    vec.tensor_tensor(ex.x[:, t.slot], bw[:], xin[:, t.c % 2], ALU.add).then_inc(ex.s_x, 1)
                    ex.dve_stats(dve, t)
                t = s.back(1)
                if t.exists(NT):
                    ex.dve_top(dve, t, hl)
                t = s.back(2)
                if t.exists(NT):
                    ex.dve_sum(dve, t, bu)
                    dve.wait_ge(ex.s_x2, t.times(1, 1))
                    vec.bn_stats(st2[:, t.slot], ex.x2[:, t.slot]).then_inc(s_st2, 1)
                    wait_alone(dve, s_st2, t.times(2, 1), mark_dve)
                    vec.bn_aggr(mv2[:, t.slot], st2[:, t.slot]).then_inc(s_st2, 1)
                t = s
                if t.exists(NT):
                    ex.dve_norm(dve, t)
                t = s.back(3)
                if t.exists(NT):
                    i = t.c % 2
                    dve.wait_ge(s_k, t.times(1, 1))
                    if t.past(2):
                        dve.wait_ge(s_acc, t.times(1, -1))
                    vec.tensor_tensor(k[:, i], b0[:], bin_[:, E:2 * E], ALU.add).then_inc(s_kb, 1)
                    dve.wait_ge(s_v, t.times(1, 1))
                    vec.tensor_tensor(v[:, i], b1[:], bin_[:, 2 * E:3 * E], ALU.add).then_inc(s_vb, 1)
                t = s.back(1)
                if t.exists(NT):
                    ex.dve_gate(dve, t, hl)
                t = s.back(2)
                if t.exists(NT):
                    dve.wait_ge(s_rr, t.times(5, 5))
                    if t.past(2):
                        dve.wait_ge(s_res, t.times(2, -2))
                        dve.wait_ge(s_t2, t.times(1, -1))
                    vec.tensor_scalar(n2[:, t.c % 2], ex.x2[:, t.slot], mv2[:, t.slot, 0:1], r1[:, t.slot],
                                      ALU.subtract, ALU.mult).then_inc(s_n2, 1)
                    vec.tensor_scalar(h2[:, t.c % 2], ex.x2[:, t.slot], mv2[:, t.slot, 0:1], r12[:, t.slot],
                                      ALU.subtract, ALU.mult).then_inc(s_h2, 1)
                t = s.back(3)
                if t.exists(NT):
                    i = t.c % 2
                    dve.wait_ge(s_q, t.times(1, 1))
                    if t.past(2):
                        dve.wait_ge(s_tq, t.times(1, -1))
                    vec.tensor_tensor(q[:, i], b0[:], bin_[:, 0:E], ALU.add).then_inc(s_qb, 1)
                t = s.back(3)
                if t.exists(NT):
                    i = t.c % 2
                    dve.wait_ge(s_rope, t.times(8, 4))
                    dve.wait_ge(s_ss, t.times(1, 1))
                    dve.wait_ge(s_vb, t.times(1, 1))
                    vec.tensor_tensor(k[:, i], k[:, i], v[:, i], ALU.mult).then_inc(s_kv, 1)
                if s.reg is None and s.c == 1:
                    dve.wait_ge(s_constb, 16 * NCONSTB)
                    vec.tensor_copy(lnbb[:], lnb[:].rearrange("p (c o) -> p c o", o=1).broadcast_to([P, KC, P]))\
                        .then_inc(s_prep, 1)
                if s.reg is None and s.c == 2:
                    for n, b in enumerate((b0, b1, ba)):
                        dve.wait_ge(s_bias, n + 1)
                        vec.tensor_tensor(bin_[:, n * E:(n + 1) * E], bin_[:, n * E:(n + 1) * E], b[:], ALU.add)\
                            .then_inc(s_fold2, 1)
                    for c in range(KC):
                        vec.tensor_scalar(win[:, c], win[:, c], lnw[:, c:c + 1], None, ALU.mult).then_inc(s_fold2, 1)
                    dve.wait_ge(s_fold2, 3 + KC)
            steps(dve, NT, R, 2 * R, NT + 4, body)
            dve.wait_ge(s_acc, NT)
            vec.tensor_copy(arow[:], ba[0:B, :]).then_inc(s_tail, 1)
            dve.wait_ge(s_tail, 2)
            vec.tensor_copy(acol[:], t1[:, 0:KC * B].rearrange("p (c b) -> p c b", b=B)).then_inc(s_tail, 1)
            dve.wait_ge(s_tail, 3)
            for b in range(B):
                for c in range(KC):
                    vec.tensor_scalar(wab[:, b, c], wout[:, c], acol[:, c, b:b + 1], None, ALU.mult)\
                        .then_inc(s_tail, 1)

        @block.scalar
        def _(act):
            nc.scalar.preload_act_table_set("exp_and_others")

            def body(s):
                t = s.back(1)
                if t.exists(NT):
                    ex.act_n1T(act, t, t0)
                t = s.back(3)
                if t.exists(NT):
                    act.wait_ge(s_t2, t.times(1, 1))
                    if t.past(2):
                        act.wait_ge(s_q, t.times(1, -1))
                    nc.scalar.copy(hT[:, t.c % 2], t1[:]).then_inc(s_hT, 1)
                t = s.back(2)
                if t.exists(NT):
                    ex.act_gaT(act, t, t1)
                t = s.back(1)
                if t.exists(NT):
                    ex.act_exps(act, t, hl)
                t = s.back(3)
                if t.exists(NT):
                    act.wait_ge(s_kb, t.times(1, 1))
                    if t.past(1):
                        act.wait_ge(s_ss, t.times(1))
                    if t.past(2):
                        act.wait_ge(s_wr, t.times(1, -1))
                    nc.scalar.activation(sq[:], k[:, t.c % 2], ACT.Square, accum_out=ss[:, t.c % 2]).then_inc(s_ss, 1)
                t = s.back(4)
                if t.exists(NT):
                    act.wait_ge(s_tq, t.times(1, 1))
                    if t.reused(2):
                        act.wait_ge(s_qTd[t.c % 2], by2(t, 16))
                    nc.scalar.copy(qT[:, t.c % 2].rearrange("p c t -> p (c t)"), t0[:]).then_inc(s_qT, 1)
                    act.wait_ge(s_qT, t.times(1, 1))
                    act.dma_start(qt_scr[bass.ds(t.times(1), 1)].rearrange("a p c t -> p (a c) t"), qT[:, t.c % 2])\
                        .then_inc(s_qTd[t.c % 2], 16)
            steps(act, NT, R, 2 * R, NT + 4, body)
            for i in range(2):
                act.wait_ge(s_qTd[i], 16 * (NT // 2))

        @block.gpsimd
        def _(pool):
            g = nc.gpsimd
            ex.pool_start(pool)

            def rotate(t, x, base):
                i = t.c % 2
                ch = Chain(pool, s_rope, t, 8, mark_pool)
                ch.n = base
                left = x[:, i, 0:NROPE]
                pairs = left.rearrange("p (n two) -> p n two", two=2)
                swp = sw[:].rearrange("p (n two) -> p n two", two=2)
                sn = rope[:, i, 1].rearrange("p (n two) -> p n two", two=2)
                ch.link(g.tensor_tensor(swp[:, :, 0], pairs[:, :, 1], sn[:, :, 0], ALU.mult))
                ch.link(g.tensor_tensor(swp[:, :, 1], pairs[:, :, 0], sn[:, :, 1], ALU.mult))
                ch.link(g.tensor_tensor(left, left, rope[:, i, 0], ALU.mult))
                ch.link(g.tensor_tensor(left, left, sw[:], ALU.add))

            def body(s):
                t = s
                if t.exists(NT):
                    ex.pool_rstd(pool, t)
                t = s.back(2)
                if t.exists(NT):
                    ch = Chain(pool, s_rr, t, 5, mark_pool)
                    wait_alone(pool, s_st2, t.times(2, 2), mark_pool)
                    if t.past(3):
                        wait_alone(pool, s_h2, t.times(1, -2), mark_pool)
                    var = mv2[:, t.slot, 1:2]
                    x1, x2, x3 = r1[:, t.slot], v2[:, t.slot], r12[:, t.slot]
                    ch.link(g.tensor_scalar(x1, var, EPS, None, ALU.add))
                    ch.link(g.tensor_tensor(x1, x1, ex.half[:], ALU.pow))
                    ch.link(g.tensor_scalar(x2, var, x1, x1, ALU.mult, ALU.mult))
                    ch.link(g.tensor_scalar(x2, x2, EPS, None, ALU.add))
                    g.tensor_tensor(x2, x2, ex.half[:], ALU.pow).then_inc(s_rrc, 1)
                    wait_alone(pool, s_rrc, t.times(1, 1), mark_pool)
                    ch.link(g.tensor_tensor(x3, x1, x2, ALU.mult))
                t = s.back(3)
                if t.exists(NT):
                    i = t.c % 2
                    pool.dma_start(rope[:, i], a["c_rope"].rearrange("(n p) (two e) -> n p two e", p=P, two=2)
                                   [bass.ds(modulo(pool, t), 1)].rearrange("n p two e -> p (n two) e"))\
                        .then_inc(s_ropein, 16)
                    wait_alone(pool, s_ropein, t.times(16, 16), mark_pool)
                    wait_alone(pool, s_ss, t.times(1, 1), mark_pool)
                    rotate(t, k, 0)
                    wait_alone(pool, s_qb, t.times(1, 1), mark_pool)
                    rotate(t, q, 4)
                    pool.sem_inc(s_qr, 1)
                    ch = Chain(pool, s_wrc, t, 1, mark_pool)
                    if t.past(2):
                        wait_alone(pool, s_acc, t.times(1, -1), mark_pool)
                    ch.link(g.tensor_tensor(rinv[:, i], ss[:, i], ex.half[:], ALU.pow))
                    g.tensor_tensor(wr[:, i], which[:, bass.ds(t.times(1), 1)].rearrange("p t b -> p (t b)"),
                                    rinv[:, i].broadcast_to([P, B]), ALU.mult).then_inc(s_wr, 1)
                    wait_alone(pool, s_wr, t.times(1, 1), mark_pool)
                t = s.back(2)
                if t.exists(NT):
                    wait_alone(pool, s_n2, t.times(1, 1), mark_pool)
                    if t.reused(R):
                        wait_alone(pool, s_resd[t.slot], t.round(16), mark_pool)
                    g.tensor_tensor(res[:, t.slot], ex.x2[:, t.slot], n2[:, t.c % 2], ALU.add).then_inc(s_res, 1)
                    wait_alone(pool, s_res, t.times(2, 1), mark_pool)
                    g.tensor_tensor(res[:, t.slot], res[:, t.slot], bout[:], ALU.add).then_inc(s_res, 1)
                    wait_alone(pool, s_res, t.times(2, 2), mark_pool)
                    pool.dma_start(res_scr[bass.ds(t.times(1), 1)].rearrange("a p e -> p (a e)"), res[:, t.slot])\
                        .then_inc(s_resd[t.slot], 16)
            pool.wait_ge(s_constb, 16 * NCONSTB)
            steps(pool, NT, R, 2 * R, NT + 4, body)
            for i in range(R):
                pool.wait_ge(s_resd[i], 16 * (NT // R))



def last(nc, a, out_tiles, qt_scr, res_scr, w):
    with ExitStack() as ctx:
        def sb(name, shape, dt=F32):
            return ctx.enter_context(nc.sbuf_tensor("l_" + name, shape, dt))

        def sem(name):
            return ctx.enter_context(nc.semaphore("l_" + name))
        mark_sp, mark_pool, mark_dve = (sem(f"l_mark_{e}") for e in ("sp", "pool", "dve"))

        def bank(name):
            return ctx.enter_context(nc.psum_tensor("l_" + name, [P, E], F32))
        ex = Experts(nc, ctx, "l_", w, mark_pool, mark_dve)
        qT, res = sb("qT", [P, R, KC, P]), sb("res", [P, R, E])
        z = [bank("z0"), bank("z1")]
        t0, t1, hl, bu = bank("t0"), bank("t1"), bank("hl"), bank("bu")
        s_in = [sem(f"in{i}") for i in range(R)]
        s_z = sem("z")
        s_out = [sem(f"out{i}") for i in range(R)]
        block = ctx.enter_context(nc.Block())

        @block.sync
        def _(sp):
            def body(t):
                if t.past(R):
                    sp.wait_ge(ex.s_x, t.times(1, 1 - R))
                sp.dma_start(qT[:, t.slot], qt_scr[bass.ds(t.times(1), 1)].rearrange("a p c t -> p (a c) t"))\
                    .then_inc(s_in[t.slot], 16)
                sp.dma_start(res[:, t.slot], res_scr[bass.ds(t.times(1), 1)].rearrange("a p e -> p (a e)"))\
                    .then_inc(s_in[t.slot], 16)
            steps(sp, NT, R, 2 * R, NT, body)

        @block.tensor
        def _(pe):
            def body(s):
                t = s
                if t.exists(NT):
                    pe.wait_ge(s_in[t.slot], t.round(32, 32))
                    if t.past(2):
                        pe.wait_ge(ex.s_x, t.times(1, -1))
                    b = t.c // TB if t.reg is None else pe.snap(t.times(1)) // TB
                    for c in range(KC):
                        rhs = w["wab"][:, bass.ds(b, 1), c].rearrange("p b e -> p (b e)")
                        mm = nc.tensor.matmul(z[t.c % 2][:], qT[:, t.slot, c], rhs, start=(c == 0), stop=(c == KC - 1))
                    mm.then_inc(s_z, 1)
                t = s.back(1)
                if t.exists(NT):
                    if t.past(1):
                        pe.wait_ge(ex.s_n1T, t.times(1))
                    ex.pe_turn(pe, t, t0)
                t = s.back(2)
                if t.exists(NT):
                    if t.past(1):
                        pe.wait_ge(ex.s_gaT, t.times(1))
                    ex.pe_turn_ga(pe, t, t1)
                t = s.back(1)
                if t.exists(NT):
                    ex.pe_down(pe, t, hl)
                t = s.back(2)
                if t.exists(NT):
                    ex.pe_up(pe, t, bu)
            steps(pe, NT, R, 2 * R, NT + 2, body)

        @block.vector
        def _(dve):
            def body(s):
                t = s
                if t.exists(NT):
                    dve.wait_ge(s_z, t.times(1, 1))
                    if t.past(R):
                        dve.wait_ge(ex.s_x2, t.times(1, 1 - R))
                    nc.vector.tensor_tensor(ex.x[:, t.slot], z[t.c % 2][:], res[:, t.slot], ALU.add)\
                        .then_inc(ex.s_x, 1)
                    ex.dve_stats(dve, t)
                t = s.back(1)
                if t.exists(NT):
                    ex.dve_top(dve, t, hl)
                t = s.back(2)
                if t.exists(NT):
                    if t.reused(R):
                        dve.wait_ge(s_out[t.slot], t.round(16))
                    ex.dve_sum(dve, t, bu)
                t = s
                if t.exists(NT):
                    ex.dve_norm(dve, t)
                t = s.back(1)
                if t.exists(NT):
                    ex.dve_gate(dve, t, hl)
            steps(dve, NT, R, 2 * R, NT + 2, body)

        @block.scalar
        def _(act):
            def body(s):
                t = s.back(1)
                if t.exists(NT):
                    ex.act_n1T(act, t, t0)
                t = s.back(2)
                if t.exists(NT):
                    ex.act_gaT(act, t, t1)
                t = s.back(1)
                if t.exists(NT):
                    ex.act_exps(act, t, hl)
            steps(act, NT, R, 2 * R, NT + 2, body)

        @block.gpsimd
        def _(pool):
            ex.pool_start(pool)

            def body(s):
                t = s
                if t.exists(NT):
                    ex.pool_rstd(pool, t)
                t = s.back(2)
                if t.exists(NT):
                    wait_alone(pool, ex.s_x2, t.times(1, 1), mark_pool)
                    pool.dma_start(out_tiles[bass.ds(t.times(1), 1)].rearrange("a p e -> p (a e)"),
                                   ex.x2[:, t.slot]).then_inc(s_out[t.slot], 16)
            steps(pool, NT, R, 2 * R, NT + 2, body)
            for i in range(R):
                pool.wait_ge(s_out[i], 16 * (NT // R))


_SHORT = {"L0_attn_a_query": "query", "L0_attn_a_Wq": "Wq", "L0_attn_a_Wk": "Wk", "L0_attn_a_Wv": "Wv",
          "L0_attn_a_Wout": "Wout", "L0_attn_a_lambda_q1": "lambda_q1", "L0_attn_a_lambda_k1": "lambda_k1",
          "L0_attn_a_lambda_q2": "lambda_q2", "L0_attn_a_lambda_k2": "lambda_k2", "L0_attn_a_rms_weight": "rms_weight",
          "L0_attn_b_ln_w": "ln_w", "L0_attn_b_ln_b": "ln_b", "L0_attn_b_W_in": "W_in", "L0_attn_b_b_in": "b_in",
          "L0_attn_b_W_out": "W_out", "L0_attn_b_b_out": "b_out", "L0_ffn_router_w": "router_w",
          "L0_ffn_down_w": "down_w", "L0_ffn_up_w": "up_w"}


def kernel(**inputs):
    import numpy as _np
    import concourse.bacc as _bacc
    from concourse import mybir as _mybir
    from concourse.bass_utils import run_bass_kernel_spmd as _run

    nc = _bacc.Bacc("TRN2", target_bir_lowering=False, num_devices=1)
    arrays, args = {}, {}
    given = {short: inputs[name] for name, short in _SHORT.items()}
    given["down_w"] = _np.transpose(_np.asarray(given["down_w"]), (2, 0, 1))
    given["router_w"] = _np.transpose(_np.asarray(given["router_w"]))
    given["up_w"] = _np.transpose(_np.asarray(given["up_w"]), (0, 2, 1))
    for name, array in {**given, **shape_constants()}.items():
        array = _np.ascontiguousarray(array)
        arrays[f"in_{name}"] = array
        args[name] = nc.dram_tensor(f"in_{name}", array.shape, _mybir.dt.from_np(array.dtype),
                                    kind="ExternalInput").ap()
    out = nc.dram_tensor("out_0", (B, T, E), F32, kind="ExternalOutput").ap()
    build(nc, args, out)
    r = _run(nc, [arrays], core_ids=[0])
    return r.results[0]["out_0"]
```

```python
from contextlib import ExitStack

import numpy as np

import concourse.bass as bass
from concourse import mybir

F32 = mybir.dt.float32
BF16 = mybir.dt.bfloat16
F32R = mybir.dt.float32r
ALU = mybir.AluOpType
ACT = mybir.ActivationFunctionType
AX = mybir.AxisListType

B, T, E = 2, 1024, 512
P = 128
NT = B * T // P
TB = T // P
KC = E // P
H = 16
D = E // H // 2
GH = 4
G = H // GH
NP = 2 * GH
HALF = T // 2
NX, IX = 8, 16
NROPE = E // 2
EPS = 1e-5
LAMBDA_INIT = 0.8 - 0.6 * float(np.exp(-0.3 * 12))
MASKED = -1e30
BAND = 32
PIECES = 6 * D
ROWS = PIECES + 3


class Step:

    def __init__(self, reg, c, stride, least=0):
        self.reg, self.c, self.stride, self.least = reg, c, stride, least

    def back(self, n):
        return Step(self.reg, self.c - n, self.stride, self.least)

    def exists(self, n):
        return self.reg is not None or 0 <= self.c < n

    def times(self, per, add=0):
        if self.reg is None:
            return self.c * per + add
        return self.reg * (self.stride * per) + (self.c * per + add)

    def reused(self, n):
        return self.reg is not None or self.c >= n

    @property
    def slot(self):
        return self.c % self.stride

    def round(self, per, add=0):
        if self.reg is None:
            return (self.c // self.stride) * per + add
        return self.reg * per + ((self.c // self.stride) * per + add)

    def past(self, n):
        if self.reg is None:
            return self.c - n >= 0
        assert self.stride * self.least + self.c >= n, (self.c, n)
        return True


def steps(eng, total, stride, first, last, body):
    for c in range(first):
        body(Step(None, c, stride))
    if total > first:
        with eng.Fori(first // stride, total // stride) as i:
            for c in range(stride):
                body(Step(i, c, stride, first // stride))
    for c in range(max(total, first), last):
        body(Step(None, c, stride))


def wait_alone(eng, sem, value, mark):
    eng.wait_ge(sem, value)
    if not isinstance(value, int):
        eng.sem_inc(mark, 1)


class Chain:

    def __init__(self, eng, sem, step, per, mark=None):
        self.eng, self.sem, self.step, self.per, self.n, self.mark = eng, sem, step, per, 0, mark

    def link(self, ins):
        self.n += 1
        ins.then_inc(self.sem, 1)
        value = self.step.times(self.per, self.n)
        if self.mark:
            wait_alone(self.eng, self.sem, value, self.mark)
        else:
            self.eng.wait_ge(self.sem, value)

    def beside(self, ins):
        self.n += 1
        ins.then_inc(self.sem, 1)

    def end(self):
        assert self.n == self.per, (self.n, self.per)



def shape_constants():
    f = np.float32
    bf = mybir.dt.np(BF16)
    inv = (f(1.0) / f(10000.0) ** (np.arange(0, D, 2, dtype=f) / f(D))).astype(f)
    ang = np.outer(np.arange(T, dtype=f), inv).astype(f)
    sign = np.where(np.arange(P) % 2 == 0, -1.0, 1.0).astype(f)
    rows = (np.arange(P) % D) // 2
    cos_a = np.cos(ang).astype(f).T[rows]
    sin_a = np.sin(ang).astype(f).T[rows] * sign[:, None]
    inv_b = (f(1.0) / f(10000.0) ** (np.arange(0, NROPE, 2, dtype=f) / f(NROPE))).astype(f)
    ang_b = np.repeat((np.arange(T, dtype=f)[:, None] * inv_b[None, :]).astype(f), 2, axis=-1)
    sgn = np.where(np.arange(NROPE) % 2 == 0, -1.0, 1.0).astype(f)
    rope_b = np.concatenate([np.cos(ang_b), np.sin(ang_b) * sgn], axis=1).astype(f)
    filt = np.exp(-0.5 * (np.linspace(0.0, 1.0, T // 2 + 1) / 0.15) ** 2)
    taps = np.fft.irfft(filt, n=T)
    u = np.arange(P + 2 * BAND)[None, :] - BAND - np.arange(P)[:, None]
    near = np.where(np.abs(u) <= BAND, taps[u % T], 0.0).astype(f)
    u = np.arange(3 * HALF)[None, :] - np.arange(P)[:, None]
    dist = np.minimum(u % T, (-u) % T)
    far = np.where(dist > BAND, taps[u % T], 0.0).astype(bf)
    i = np.arange(P)
    ident = np.eye(P, dtype=f)
    mask_s = np.where(i[None, :] > i[:, None], MASKED, 0.0).astype(bf)
    mask_t = np.ascontiguousarray(mask_s.T)
    heads = (i[:, None] // (2 * D) == i[None, :] // (2 * D)).astype(f) / (2 * D)
    tri = (np.arange(NX)[None, :] < np.arange(NX)[:, None]).astype(f).reshape(1, NX * NX)
    tri = np.broadcast_to(tri, (P, NX * NX)).copy()
    which = np.zeros((P, NT, B), f)
    which[:, np.arange(NT), np.arange(NT) // TB] = 1.0
    return {
        "c_cos": cos_a, "c_sin": sin_a, "c_rope": rope_b, "c_near": near, "c_far": far, "c_ident": ident,
        "c_identb": ident.astype(bf), "c_mask_s": mask_s, "c_mask_t": mask_t, "c_heads": heads,
        "c_tri": tri, "c_which": which.reshape(P, NT * B),
    }


def build(nc, a, out):
    x_tiles = a["query"].rearrange("b (n p) e -> (b n) p e", p=P)
    out_tiles = out.rearrange("b (n p) e -> (b n) p e", p=P)
    v_scr = nc.dram_tensor("v_scratch", (NT, P, E), F32, kind="Internal").ap()
    piece_scr = nc.dram_tensor("piece_scratch", (2, 2, 3, P, T), BF16, kind="Internal").ap()
    shift_scr = nc.dram_tensor("shift_scratch", (2, 3, NP, HALF), BF16, kind="Internal").ap()
    att_scr = nc.dram_tensor("att_scratch", (B * G, P, T), F32, kind="Internal").ap()
    qt_scr = nc.dram_tensor("qt_scratch", (NT, P, KC, P), F32, kind="Internal").ap()
    res_scr = nc.dram_tensor("res_scratch", (NT, P, E), F32, kind="Internal").ap()
    with ExitStack() as outer:
        marks = [outer.enter_context(nc.semaphore(f"mark_{e}")) for e in ("sp", "pool", "dve")]
        s_ahead = outer.enter_context(nc.semaphore("ahead"))
        ident = outer.enter_context(nc.sbuf_tensor("ident", [P, P], F32))
        xnT = outer.enter_context(nc.sbuf_tensor("xnT", [P, KC, NT * P], F32))
        rms, lnw, lnb = (outer.enter_context(nc.sbuf_tensor(n, shape, F32))
                         for n, shape in (("rms", [P, 1]), ("lnw", [P, KC]), ("lnb", [P, KC])))
        small = dict(rms=rms, lnw=lnw, lnb=lnb)
        place = xnT[:].rearrange("p c t -> p (c t)")
        win = [place[:, c * 3 * E:(c + 1) * 3 * E] for c in range(KC)]
        wo = place[:, 3 * KC * E:4 * KC * E].rearrange("p (c e) -> p c e", c=KC)
        normalise(nc, marks, a, x_tiles, v_scr, ident, xnT)
        attention(nc, marks, a, v_scr, piece_scr, shift_scr, att_scr, ident, xnT, win, wo, small, s_ahead)
        with ExitStack() as ctx:
            def sb(name, shape, dt=F32):
                return ctx.enter_context(nc.sbuf_tensor(name, shape, dt))
            w = dict(
                **small, ident=ident, tri=sb("tri", [P, NX, NX]), win=win, wo=wo,
                down=sb("down", [P, KC, NX * IX + NX]), up=sb("up", [P, E]), bout=sb("bout", [P, E]),
                wab=place[:, 0:B * KC * E].rearrange("p (b c e) -> p b c e", b=B, c=KC),
                wout=place[:, B * KC * E:(B + 1) * KC * E].rearrange("p (c e) -> p c e", c=KC),
                res=place[:, 3 * KC * E:3 * KC * E + R * E].rearrange("p (r e) -> p r e", r=R),
            )
            middle(nc, marks, a, x_tiles, att_scr, qt_scr, res_scr, w)
            last(nc, marks, a, out_tiles, qt_scr, res_scr, w)



def normalise(nc, marks, a, x_tiles, v_scr, ident, xnT):
    R = 4
    with ExitStack() as ctx:
        def sb(name, shape, dt=F32):
            return ctx.enter_context(nc.sbuf_tensor(name, shape, dt))

        def sem(name):
            return ctx.enter_context(nc.semaphore(name))
        mark_sp, mark_pool, mark_dve = marks
        wv = sb("wv", [P, KC, E])
        x = sb("x1in", [P, R, E])
        xn = sb("xn", [P, R, E])
        st = sb("st", [P, R, 6])
        mv = sb("mv", [P, R, 2])
        rstd = sb("rstd", [P, R, 1])
        mhalf = sb("mhalf", [P, 1])
        xt = sb("xt", [P, R, KC, P])
        wvh, wvl = sb("wvh", [P, KC, E], F32R), sb("wvl", [P, KC, E], F32R)
        xth, xtl = sb("xth", [P, R, KC, P], F32R), sb("xtl", [P, R, KC, P], F32R)
        v = sb("v", [P, R, E])
        tp = [ctx.enter_context(nc.psum_tensor(f"n_tp{i}", [P, E], F32)) for i in range(R)]
        vp = [ctx.enter_context(nc.psum_tensor(f"n_vp{i}", [P, E], F32)) for i in range(R)]
        s_const, s_mhalf, s_var = sem("n_const"), sem("n_mhalf"), sem("n_var")
        s_ident, s_w, s_xth, s_xtl = sem("n_ident"), sem("n_w"), sem("n_xth"), sem("n_xtl")
        s_x = [sem(f"n_x{i}") for i in range(R)]
        s_stat, s_agg, s_rstd, s_xn = sem("n_stat"), sem("n_agg"), sem("n_rstd"), sem("n_xn")
        s_tp, s_xt, s_big, s_vp, s_v = sem("n_tp"), sem("n_xt"), sem("n_big"), sem("n_vp"), sem("n_v")
        s_vout = [sem(f"n_vout{i}") for i in range(R)]
        block = ctx.enter_context(nc.Block())

        @block.sync
        def _(sp):
            def load_x(t):
                if t.past(R):
                    wait_alone(sp, s_xn, t.times(1, 1 - R), mark_sp)
                sp.dma_start(x[:, t.slot], x_tiles[bass.ds(t.times(1), 1)].rearrange("a p e -> p (a e)"))\
                    .then_inc(s_x[t.slot], 16)

            load_x(Step(None, 0, R))
            sp.dma_start(ident[:], a["c_ident"]).then_inc(s_ident, 16)
            for c in range(1, R):
                load_x(Step(None, c, R))
            sp.dma_start(wv[:], a["Wv"].rearrange("(c p) n -> p c n", p=P)).then_inc(s_const, 16)

            def body(t):
                if t.reg is not None or t.c >= R:
                    load_x(t)
            steps(sp, NT, R, 2 * R, NT, body)

        @block.vector
        def _(dve):
            def body(s):
                t = s
                if t.exists(NT):
                    dve.wait_ge(s_x[t.slot], t.round(16, 16))
                    nc.vector.bn_stats(st[:, t.slot], x[:, t.slot]).then_inc(s_stat, 1)
                    wait_alone(dve, s_stat, t.times(1, 1), mark_dve)
                    nc.vector.bn_aggr(mv[:, t.slot], st[:, t.slot]).then_inc(s_agg, 1)
                t = s.back(1)
                if t.exists(NT):
                    dve.wait_ge(s_rstd, t.times(1, 1))
                    if t.past(R):
                        dve.wait_ge(s_tp, t.times(1, 1 - R))
                    nc.vector.tensor_scalar(xn[:, t.slot], x[:, t.slot], mv[:, t.slot, 0:1], rstd[:, t.slot],
                                            ALU.subtract, ALU.mult).then_inc(s_xn, 1)
                t = s.back(2)
                if t.exists(NT):
                    dve.wait_ge(s_tp, t.times(1, 1))
                    if t.past(3):
                        dve.wait_ge(s_vp, t.times(1, -2))
                        dve.wait_ge(s_big, t.times(1, -2))
                    bank = tp[t.slot][:].rearrange("p (c t) -> p c t", c=KC)
                    dve.wait_ge(s_xth, t.times(1, 1))
                    nc.vector.tensor_copy(xt[:, t.slot], bank).then_inc(s_xt, 1)
                    dve.wait_ge(s_xt, t.times(1, 1))
                    nc.vector.tensor_tensor(xtl[:, t.slot], xt[:, t.slot], xth[:, t.slot].bitcast(F32), ALU.subtract)\
                        .then_inc(s_xtl, 1)
                if s.reg is None and s.c == 1:
                    dve.wait_ge(s_w, 1)
                    nc.vector.tensor_tensor(wvl[:], wv[:], wvh[:].bitcast(F32), ALU.subtract).then_inc(s_w, 1)
            steps(dve, NT, R, 2 * R, NT + 2, body)

        @block.gpsimd
        def _(pool):
            nc.gpsimd.memset(mhalf[:], -0.5).then_inc(s_mhalf, 1)
            pool.wait_ge(s_mhalf, 1)

            def body(s):
                t = s
                if t.exists(NT):
                    wait_alone(pool, s_agg, t.times(1, 1), mark_pool)
                    if t.past(R):
                        wait_alone(pool, s_xn, t.times(1, 1 - R), mark_pool)
                    nc.gpsimd.tensor_scalar(rstd[:, t.slot], mv[:, t.slot, 1:2], EPS, None, ALU.add).then_inc(s_var, 1)
                    wait_alone(pool, s_var, t.times(1, 1), mark_pool)
                    nc.gpsimd.tensor_tensor(rstd[:, t.slot], rstd[:, t.slot], mhalf[:], ALU.pow).then_inc(s_rstd, 1)
                t = s.back(2)
                if t.exists(NT):
                    wait_alone(pool, s_xt, t.times(1, 1), mark_pool)
                    nc.gpsimd.tensor_copy(xnT[:, :, bass.ds(t.times(P), P)], xt[:, t.slot]).then_inc(s_big, 1)
            steps(pool, NT, R, 2 * R, NT + 2, body)

        @block.tensor
        def _(pe):
            pe.wait_ge(s_ident, 16)

            def body(s):
                t = s.back(1)
                if t.exists(NT):
                    pe.wait_ge(s_xn, t.times(1, 1))
                    if t.past(R):
                        pe.wait_ge(s_xt, t.times(1, 1 - R))
                    for c in range(KC):
                        mm = nc.tensor.transpose(tp[t.slot][:, c * P:(c + 1) * P], xn[:, t.slot, c * P:(c + 1) * P],
                                                 ident[:])
                    mm.then_inc(s_tp, 1)
                t = s.back(2)
                if t.exists(NT):
                    pe.wait_ge(s_xtl, t.times(1, 1))
                    if t.reg is None and t.c == 0:
                        pe.wait_ge(s_w, 2)
                    if t.past(3):
                        pe.wait_ge(s_v, t.times(1, -2))
                    for c in range(KC):
                        for n, (x_, w_) in enumerate(((xth, wvh), (xtl, wvh), (xth, wvl))):
                            mm = nc.tensor.matmul(vp[t.slot][:], x_[:, t.slot, c], w_[:, c], start=(c == 0 and n == 0),
                                                  stop=(c == KC - 1 and n == 2))
                    mm.then_inc(s_vp, 1)
            steps(pe, NT, R, 2 * R, NT + 2, body)

        @block.scalar
        def _(act):
            def body(s):
                t = s.back(1)
                if t.exists(NT):
                    act.wait_ge(s_tp, t.times(1, 1))
                    if t.past(R):
                        act.wait_ge(s_vp, t.times(1, 1 - R))
                    nc.scalar.copy(xth[:, t.slot], tp[t.slot][:].rearrange("p (c t) -> p c t", c=KC))\
                        .then_inc(s_xth, 1)
                t = s.back(2)
                if t.exists(NT):
                    act.wait_ge(s_vp, t.times(1, 1))
                    if t.reused(R):
                        act.wait_ge(s_vout[t.slot], t.round(16))
                    nc.scalar.copy(v[:, t.slot], vp[t.slot][:]).then_inc(s_v, 1)
                    act.wait_ge(s_v, t.times(1, 1))
                    act.dma_start(v_scr[bass.ds(t.times(1), 1)].rearrange("a p e -> p (a e)"), v[:, t.slot])\
                        .then_inc(s_vout[t.slot], 16)
                if s.reg is None and s.c == 1:
                    act.wait_ge(s_const, 16)
                    nc.scalar.copy(wvh[:], wv[:]).then_inc(s_w, 1)
            steps(act, NT, R, 2 * R, NT + 2, body)
            for i in range(R):
                act.wait_ge(s_vout[i], 16 * (NT // R))



def near_windows(half):
    found = []
    for j in range(TB):
        lo, hi = j * P - BAND, (j + 1) * P + BAND
        for wrap in (-T, 0, T):
            s, e = max(lo + wrap, half * HALF), min(hi + wrap, (half + 1) * HALF)
            if s < e:
                found.append((j, s - wrap - lo, s - half * HALF, e - s))
    return found


def rows_units():
    units = []
    for i in range(TB):
        n = 2 if (i + 1) * P <= HALF else 1
        units += [(i, a, n) for a in range(0, NP, n)]
    return units


def prob_units():
    return [(h, j, w, g) for h in range(2) for j in range((h + 1) * TB // 2) for w in range(2) for g in (0, 2)]


FIRST = GH * 4
LEAD, TRAIL, NEXT_LEAD, NEXT_TRAIL = 3, 10, 1, 8
VALUES_LATER = 3
SHIFT1_LATER = 4
SHIFT0_LATER = 4
USES = {5: "turn0", 7: "turn1", 15: "low0", 22: "low1", 27: "square0", 29: "square1", "rows": "shift1",
        51: "q0", 61: "q1", 66: "k0", 74: "k1", "ahead": "shift0"}
PARTS = {"q": 4, "k": 4, "l": 6}
ROOTS = {32: 0, 49: 1}


def merge(many, few):
    out, done = [], 0
    for n, x in enumerate(many):
        out.append(x)
        while done * len(many) < (n + 1) * len(few) - len(many) // 2 and done < len(few):
            out.append(few[done])
            done += 1
    return out + few[done:]


def events(ahead):
    rows = [("rows", n) for n in range(FIRST, len(rows_units()))]
    half0 = [("probs", m) for m in range(len(prob_units()) // 3)]
    half1 = [("probs", m) for m in range(len(half0), len(prob_units()))]
    nxt = [("ahead", n) for n in range(FIRST)] if ahead else []
    cut = len(half0) - TRAIL
    slots = rows[:LEAD] + merge(rows[LEAD:], half0[:cut]) + half0[cut:]
    cut = len(half1) - NEXT_TRAIL
    slots += nxt[:NEXT_LEAD] + merge(half1[:cut], nxt[NEXT_LEAD:]) + half1[cut:]
    out, due = [], []
    for n, (kind, u) in enumerate(slots):
        out.append((kind, u))
        due = [(m, k - 1) for m, k in due]
        if kind == "probs" and u % 2:
            due.append((u, VALUES_LATER))
        while due and due[0][1] == 0:
            m = due.pop(0)[0]
            out.append(("values", m))
            if m == half0[-1][1]:
                out.append(("out", 0))
        if n == 0:
            out.append(("out", 1))
        if n in ROOTS:
            out.append(("root", ROOTS[n]))
        for end, name in USES.items():
            last = PARTS.get(name[0], 1) - 1
            if isinstance(end, int) and 0 <= n - end + last < last:
                out.append(("part", (name, n - end + last)))
        if n in USES:
            out.append(("use", USES[n]))
        if (kind, u) == rows[-1]:
            out.append(("sums", 1))
        if n == slots.index(rows[-1]) + SHIFT1_LATER:
            out.append(("use", USES["rows"]))
        if nxt and (kind, u) == nxt[-1]:
            out.append(("sums", 0))
        if nxt and n == slots.index(nxt[-1]) + SHIFT0_LATER:
            out.append(("use", USES["ahead"]))
    return out + [("values", m) for m, _ in due]


SLOTS = ("rows", "ahead", "probs")
NSLOT = 3
NPROB = 6


def attention(nc, marks, a, v_scr, piece_scr, shift_scr, att_scr, ident, xnT, win, wo, small, s_ahead):
    NG = B * G
    RU, PU = rows_units(), prob_units()
    NU, NQ = len(RU), len(PU)
    UN = NU + NQ
    EVENTS = {ahead: events(ahead) for ahead in (True, False)}
    NV = NQ // 2
    SH = 4
    with ExitStack() as ctx:
        def sb(name, shape, dt=F32):
            return ctx.enter_context(nc.sbuf_tensor(name, shape, dt))

        def sem(name):
            return ctx.enter_context(nc.semaphore(name))
        mark_sp, mark_pool, mark_dve = marks
        cos, sin = sb("cos", [P, T]), sb("sin", [P, T])
        near = sb("near", [P, P + 2 * BAND])
        far = sb("far", [P, 3 * HALF], BF16)
        identb = sb("identb", [P, P], BF16)
        mask_s, mask_t = sb("mask_s", [P, P], BF16), sb("mask_t", [P, P], BF16)
        headsum = sb("headsum", [P, P])
        lam_in = sb("lam_in", [P, 4, D])
        lam_p = sb("lam_p", [P, 2, D])
        lam_e = sb("lam_e", [P, 2, 1])
        nlam = sb("nlam", [P, 1])
        wg = sb("wg", [P, 2, KC, 2, P])
        vg = sb("vg", [P, 2, TB, P])
        vn = sb("vn", [P, 2, TB, P])
        qst, kst = sb("qst", [P, 2, NP, T], BF16), sb("kst", [P, 2, NP, T], BF16)
        raw = sb("raw", [P, T])
        swapped = sb("swapped", [P, T])
        rot = sb("rot", [P, T])
        pieces = sb("pieces", [P, 2, 3, T], BF16)
        prob = sb("prob", [P, NPROB, 2, HALF])
        nmax, den = sb("nmax", [P, NP, TB]), sb("den", [P, NP, TB])
        shift, rest = sb("shift", [P, NP, TB]), sb("rest", [P, NP, TB])
        shp = sb("shp", [P, TB, 3, NP], BF16)
        shrow = sb("shrow", [3 * NP, 2, HALF], BF16)
        oT = sb("oT", [P, T])
        onat = sb("onat", [P, TB, P])
        onb = sb("onb", [P, TB, P], BF16)
        y = sb("y", [P, T])
        sq = sb("sq", [P, T])
        rs = sb("rs", [P, HALF])
        newton = sb("newton", [P, HALF])

        score = [ctx.enter_context(nc.psum_tensor(f"score{i}", [P, 2, HALF], F32)) for i in range(NSLOT)]
        acc = ctx.enter_context(nc.psum_tensor("acc", [P, HALF], F32))
        misc = ctx.enter_context(nc.psum_tensor("misc", [P, HALF], F32))
        miscb = misc[:].bitcast(BF16)

        s_const, s_lam, s_turn = sem("a_const"), sem("a_lam"), sem("a_turn")
        s_wg = [sem(f"a_wg{i}") for i in range(2)]
        s_vg = [sem(f"a_vg{i}") for i in range(2)]
        s_vn = sem("a_vn")
        s_slot, s_max, s_exp = sem("a_slot"), sem("a_max"), sem("a_exp")
        s_misc, s_mread = sem("a_misc"), sem("a_mread")
        s_swap, s_cosm, s_rot, s_chain = sem("a_swap"), sem("a_cosm"), sem("a_rot"), sem("a_chain")
        s_piece = [sem(f"a_piece{i}") for i in range(2)]
        s_stack = [[sem(f"a_stack{w}{i}") for i in range(2)] for w in range(2)]
        s_ln, s_sh, s_shrow = sem("a_ln"), sem("a_sh"), sem("a_shrow")
        s_shdma = [sem(f"a_shdma{h}") for h in range(2)]
        s_shout = [sem(f"a_shout{h}") for h in range(2)]
        s_pv, s_oT, s_ones = sem("a_pv"), sem("a_oT"), sem("a_ones")
        s_nat, s_y, s_sq, s_rs, s_att = sem("a_nat"), sem("a_y"), sem("a_sq"), sem("a_rs"), sem("a_att")
        s_newton = sem("a_newton")
        s_attdma = sem("a_attdma")
        block = ctx.enter_context(nc.Block())

        order = [u for kind, u in EVENTS[True] if kind == "use"]
        NM = len(order)
        LOWPASS = [u for u in order if u[:3] in ("tur", "low", "squ")]
        PROJECT = ["q0", "q1", "k0", "k1"]
        BEFORE = [(0, u) for u in PROJECT] + [(1, u) for u in PROJECT[:2]] + [(0, "shift0")] + \
            [(1, u) for u in PROJECT[2:]]

        def step_uses(c):
            return [u for u in order if not (u in LOWPASS and c < 1 or u in PROJECT and c >= NG - 2 or
                                             u == "shift0" and c == NG - 1)]

        def use_in(g, name):
            if g.reg is None:
                return len(BEFORE) + sum(len(step_uses(c)) for c in range(g.c)) + step_uses(g.c).index(name) + 1
            return g.times(NM, len(BEFORE) + len(step_uses(0)) - NM + order.index(name) + 1)

        def use0(group, name):
            return BEFORE.index((group, name)) + 1

        def final_use(name):
            return len(BEFORE) + sum(len(step_uses(c)) for c in range(NG)) + LOWPASS.index(name) + 1

        first, second = Step(None, 0, 2), Step(None, 1, 2)

        def is_more(g, n):
            return g.reg is not None or g.c < NG - n

        def step_events(g):
            n, out = -1, []
            for kind, u in EVENTS[is_more(g, 1)]:
                if kind in SLOTS:
                    n += 1
                name = u[0] if kind == "part" else u
                if kind in ("use", "part") and (name in PROJECT and not is_more(g, 2) or name in LOWPASS and not g.past(1)):
                    continue
                if kind in ("out", "root") and not g.past(1) and (kind, u) != ("out", 0):
                    continue
                out.append((kind, u, n))
            return out

        place = {(kind, u): n for kind, u, n in step_events(Step(None, 1, 2)) if kind in SLOTS}
        final_place = {(kind, u): n for kind, u, n in step_events(Step(None, NG - 1, 2)) if kind in SLOTS}

        def count(g, n):
            return g.times(UN, FIRST + n + 1)

        def place_of(g, kind, u):
            return (final_place if g.reg is None and g.c == NG - 1 else place)[kind, u]

        def halves(name):
            return int(name[-1])

        def group_steps(eng, body):
            steps(eng, NG - 2, 2, 2, NG, body)

        def batch(eng, g):
            if g.reg is None:
                return g.c // G
            return eng.snap(g.times(1)) // G

        def column(eng, g):
            if g.reg is None:
                return (g.c % G) * P
            return (eng.snap(g.times(1)) % G) * P

        @block.sync
        def _(sp):
            def load_w(g):
                col = column(sp, g)
                for n, name in enumerate(("Wq", "Wk")):
                    sp.dma_start(wg[:, g.slot, :, n],
                                 a[name].rearrange("(c p) n -> p c n", p=P)[:, :, bass.ds(col, P)])\
                        .then_inc(s_wg[g.slot], 16)

            def load_v(g):
                if g.past(2):
                    wait_alone(sp, s_pv, g.times(NV, -NV), mark_sp)
                b8 = batch(sp, g) * TB
                sp.dma_start(vg[:, g.slot], v_scr[bass.ds(b8, TB), :, bass.ds(column(sp, g), P)]
                             .rearrange("s p e -> p s e")).then_inc(s_vg[g.slot], 16)

            def stack(g, w):
                wait_alone(sp, s_piece[w], g.times(16, 16), mark_sp)
                if g.past(2):
                    wait_alone(sp, s_pv, g.times(NV, -NV), mark_sp)
                for n, piece in enumerate(((0, 1, 2, 0, 1, 0), (0, 0, 0, 1, 1, 2))[w]):
                    sp.dma_start((qst, kst)[w][n * D:(n + 1) * D, g.slot],
                                 piece_scr[g.slot, w, piece].rearrange("(a d) t -> d a t", d=D))\
                        .then_inc(s_stack[w][g.slot], 16)

            def shift_in(g, h):
                wait_alone(sp, s_shrow, g.times(2, h + 1), mark_sp)
                sp.dma_start(shift_scr[h].rearrange("n a t -> (n a) t"), shrow[:, h]).then_inc(s_shout[h], 16)
                wait_alone(sp, s_shout[h], g.times(16, 16), mark_sp)
                sp.dma_start(qst[PIECES:ROWS, g.slot, :, h * HALF:(h + 1) * HALF], shift_scr[h])\
                    .then_inc(s_shdma[h], 16)

            def store(g):
                wait_alone(sp, s_att, g.times(2, 2), mark_sp)
                sp.dma_start(att_scr[bass.ds(g.times(1), 1)].rearrange("g p t -> p (g t)"), y[:]).then_inc(s_attdma, 16)

            load_w(first)
            for dst, src in ((cos, "c_cos"), (sin, "c_sin")):
                sp.dma_start(dst[:], a[src]).then_inc(s_turn, 16)
            for dst, src in ((near, "c_near"), (far, "c_far"), (identb, "c_identb"),
                             (mask_s, "c_mask_s"), (mask_t, "c_mask_t"), (headsum, "c_heads")):
                sp.dma_start(dst[:], a[src]).then_inc(s_const, 16)
            for n, name in enumerate(("lambda_q1", "lambda_k1", "lambda_q2", "lambda_k2")):
                sp.dma_start(lam_in[:, n], a[name].rearrange("(o d) -> o d", o=1).broadcast_to([P, D]))\
                    .then_inc(s_const, 16)
            load_w(second)
            load_v(first)
            for w in range(2):
                stack(first, w)
            shift_in(first, 0)

            def weights_ahead():
                sp.wait_ge(s_mread, use_in(Step(None, NG - 3, 2), "k1"))
                for c in range(KC):
                    sp.dma_start(win[c], a["W_in"].rearrange("(c p) n -> c p n", p=P)[c]).then_inc(s_ahead, 16)
                sp.dma_start(wo, a["Wout"].rearrange("(c p) n -> p c n", p=P)).then_inc(s_ahead, 16)
                for n in range(GH):
                    sp.dma_start(small["rms"][n * 2 * D:(n + 1) * 2 * D],
                                 a["rms_weight"].rearrange("(p o) -> p o", o=1)).then_inc(s_ahead, 16)
                for name, src in (("lnw", "ln_w"), ("lnb", "ln_b")):
                    sp.dma_start(small[name][:], a[src].rearrange("(c p) -> p c", p=P),
                                 allow_slow_non_contiguous=True).then_inc(s_ahead, 16)

            def body(g):
                if g.reg is None and g.c == NG - 1:
                    weights_ahead()
                if is_more(g, 2):
                    wait_alone(sp, s_mread, use_in(g.back(2), "k1") if g.past(2) else use0(g.c, "k1"), mark_sp)
                    load_w(g.back(-2))
                if is_more(g, 1):
                    stack(g.back(-1), 0)
                    load_v(g.back(-1))
                    stack(g.back(-1), 1)
                shift_in(g, 1)
                if g.past(1):
                    store(g.back(1))
                if is_more(g, 1):
                    shift_in(g.back(-1), 0)

            group_steps(sp, body)
            store(Step(None, NG - 1, 2))
            sp.wait_ge(s_attdma, 16 * NG)
            sp.wait_ge(s_ahead, 16 * (KC + 1 + GH + 2))

        @block.tensor
        def _(pe):
            def take(number):
                if isinstance(number, int) and number < 2:
                    return
                pe.wait_ge(s_mread, number - 1)

            def project(g, name, number, parts):
                h, w = halves(name), int(name[0] == "k")
                if 0 in parts:
                    pe.wait_ge(s_wg[g.slot], g.round(32, 32))
                    take(number)
                base = batch(pe, g) * T + h * HALF
                for c in parts:
                    mm = nc.tensor.matmul(misc[:], wg[:, g.slot, c, w], xnT[:, c, bass.ds(base, HALF)],
                                          start=(c == 0), stop=(c == KC - 1))
                if KC - 1 in parts:
                    mm.then_inc(s_misc, 1)

            def lowpass(g, name, number, parts):
                h = halves(name)
                if 0 in parts:
                    take(number)
                if name[0] == "t":
                    pe.wait_ge(s_oT, g.times(2, 2))
                    for i in range(4):
                        j = 4 * h + i
                        mm = nc.tensor.transpose(misc[:, i * P:(i + 1) * P], oT[:, j * P:(j + 1) * P], ident[:])
                elif name[0] == "l":
                    if 0 in parts:
                        pe.wait_ge(s_nat, g.times(4, 4))
                    for j in range(TB):
                        if j // 2 in parts:
                            off = (h * HALF - j * P) % T
                            nc.tensor.matmul(misc[:], onb[:, j], far[:, off:off + HALF], start=(j == 0),
                                             stop=(j == TB - 1), skip_group_check=True)
                    win = near_windows(h)
                    for n, (j, col, t0, cnt) in enumerate(win):
                        if (4 if n < len(win) // 2 else 5) in parts:
                            mm = nc.tensor.matmul(misc[:, t0:t0 + cnt], onat[:, j], near[:, col:col + cnt],
                                                  start=False, stop=True, skip_group_check=True)
                else:
                    pe.wait_ge(s_sq, g.times(2, h + 1))
                    mm = nc.tensor.matmul(misc[:], headsum[:], sq[:, h * HALF:(h + 1) * HALF], start=True, stop=True)
                if name[0] != "l" or PARTS["l"] - 1 in parts:
                    mm.then_inc(s_misc, 1)

            def shifts(g, name, number):
                h = halves(name)
                take(number)
                pe.wait_ge(s_sh, g.times(2, h + 1))
                for i in range(SH):
                    mm = nc.tensor.transpose(miscb[0:3 * NP, i * P:(i + 1) * P],
                                             shp[:, h * SH + i].rearrange("p a b -> p (a b)"), identb[:])
                mm.then_inc(s_misc, 1)

            def slot_free(number):
                if not isinstance(number, int) or number > NSLOT:
                    pe.wait_ge(s_exp, number - NSLOT)

            def rows(g, u, number, slot):
                i, pair, cnt = RU[u]
                slot_free(number)
                width = (i + 1) * P
                for k in range(cnt):
                    for c0 in range(0, width, HALF):
                        w = min(HALF, width - c0)
                        bank = k if cnt == 2 else c0 // HALF
                        diag = c0 + w == width
                        mm = nc.tensor.matmul(score[slot][:, bank, 0:w],
                                              qst[0:PIECES, g.slot, pair + k, i * P:(i + 1) * P],
                                              kst[0:PIECES, g.slot, pair + k, c0:c0 + w], start=True, stop=True)
                        if diag:
                            mm = nc.tensor.matmul(score[slot][:, bank, w - P:w], identb[:], mask_s[:],
                                                  start=False, stop=True, skip_group_check=True)
                mm.then_inc(s_slot, 1)

            def probs(g, m, number, slot):
                h, j, which, head = PU[m]
                slot_free(number)
                t0 = max(j * P - h * HALF, 0)
                for k in range(2):
                    pair = 2 * (head + k) + which
                    diag = j >= 4 * h
                    mm = nc.tensor.matmul(score[slot][:, k, t0:HALF], kst[0:ROWS, g.slot, pair, j * P:(j + 1) * P],
                                          qst[0:ROWS, g.slot, pair, h * HALF + t0:(h + 1) * HALF],
                                          start=True, stop=True)
                    if diag:
                        mm = nc.tensor.matmul(score[slot][:, k, t0:t0 + P], identb[:], mask_t[:],
                                              start=False, stop=True, skip_group_check=True)
                mm.then_inc(s_slot, 1)

            def values(g, m):
                h, j, which, _ = PU[m]
                pe.wait_ge(s_exp, count(g, place_of(g, "probs", m)))
                t0 = max(j * P - h * HALF, 0)
                if j == 0 and which == 0:
                    if g.reg is not None or g.c > 0 or h:
                        pe.wait_ge(s_oT, g.times(2, h))
                end = j == (h + 1) * TB // 2 - 1 and which == 1
                for head in range(GH):
                    pslot = (m - 1 + head // 2) % NPROB
                    v = (vg, vn)[which]
                    mm = nc.tensor.matmul(acc[head * 32:head * 32 + 32, t0:HALF],
                                          v[:, g.slot, j, head * 32:head * 32 + 32],
                                          prob[:, pslot, head % 2, t0:HALF],
                                          start=(j == 0 and which == 0), stop=end, skip_group_check=True)
                mm.then_inc(s_pv, 1)

            def stacks_in(g):
                for w in range(2):
                    pe.wait_ge(s_stack[w][g.slot], g.round(96, 96))

            for g, names in ((first, PROJECT), (second, PROJECT[:2])):
                for name in names:
                    project(g, name, use0(g.c, name), range(KC))
            pe.wait_ge(s_const, 16 * 10)
            stacks_in(first)
            for n in range(FIRST):
                rows(first, n, n + 1, n % NSLOT)
            shifts(first, "shift0", use0(0, "shift0"))
            for name in PROJECT[2:]:
                project(second, name, use0(1, name), range(KC))

            def body(g):
                for kind, u, n in step_events(g):
                    number, slot = count(g, n), (FIRST + n) % NSLOT
                    if kind == "rows":
                        rows(g, u, number, slot)
                    elif kind == "ahead":
                        if u == 0:
                            stacks_in(g.back(-1))
                        rows(g.back(-1), u, number, slot)
                    elif kind == "probs":
                        if u == 0:
                            pe.wait_ge(s_vg[g.slot], g.round(16, 16))
                            pe.wait_ge(s_vn, g.times(1, 1))
                            pe.wait_ge(s_ones, 1)
                            pe.wait_ge(s_shdma[0], g.times(16, 16))
                        elif PU[u][0] != PU[u - 1][0]:
                            pe.wait_ge(s_shdma[1], g.times(16, 16))
                        probs(g, u, number, slot)
                    elif kind == "values":
                        values(g, u)
                    elif kind in ("use", "part"):
                        name, part = u if kind == "part" else (u, PARTS.get(u[0], 1) - 1)
                        if name in PROJECT:
                            project(g.back(-2), name, use_in(g, name), (part,))
                        elif name in LOWPASS:
                            lowpass(g.back(1), name, use_in(g, name), (part,))
                        else:
                            shifts(g.back(-1) if name == "shift0" else g, name, use_in(g, name))
            group_steps(pe, body)
            for name in LOWPASS:
                lowpass(Step(None, NG - 1, 2), name, final_use(name), range(PARTS.get(name[0], 1)))

        @block.vector
        def _(dve):
            def project(g, name, number):
                h, w = halves(name), int(name[0] == "k")
                cols = slice(h * HALF, (h + 1) * HALF)
                dve.wait_ge(s_misc, number)
                if w or g.past(1):
                    dve.wait_ge(s_cosm, g.times(2, w))
                nc.vector.tensor_scalar(raw[:, cols], misc[:], (1.0, float(D) ** -0.5)[w], None, ALU.mult)\
                    .then_inc(s_mread, 1)
                if h == 1:
                    wait_alone(dve, s_mread, number, mark_dve)
                    if w or g.past(1):
                        wait_alone(dve, s_rot, g.times(12, 6 * w - 4), mark_dve)
                    nc.vector.stream_shuffle(swapped[:], raw[:], [i ^ 1 for i in range(32)])\
                        .then_inc(s_swap, 1)

            def lowpass(g, name, number):
                h = halves(name)
                cols = slice(h * HALF, (h + 1) * HALF)
                dve.wait_ge(s_misc, number)
                if name[0] == "t":
                    dst, dstb = onat[:, 4 * h:4 * h + 4], onb[:, 4 * h:4 * h + 4]
                    src = misc[:].rearrange("p (j c) -> p j c", j=4)
                    nc.vector.tensor_copy(dst, src).then_inc(s_nat, 1)
                    nc.vector.tensor_copy(dstb, src).then_inc(s_nat, 1)
                    dve.wait_ge(s_nat, g.times(4, 2 * h + 2))
                    dve.sem_inc(s_mread, 1)
                elif name[0] == "l":
                    if g.past(1):
                        dve.wait_ge(s_attdma, g.times(16))
                    nc.vector.tensor_copy(y[:, cols], misc[:]).then_inc(s_y, 1)
                    dve.wait_ge(s_y, g.times(2, h + 1))
                    dve.sem_inc(s_mread, 1)
                else:
                    dve.wait_ge(s_sq, g.times(2, h + 1))
                    nc.vector.tensor_scalar(sq[:, cols], misc[:], EPS, None, ALU.add).then_inc(s_mread, 1)

            def shift_pieces(g, h):
                c = slice(h * SH, (h + 1) * SH)
                ch = Chain(dve, s_chain, g, 10)
                ch.n = 5 * h
                dve.wait_ge(s_ln, g.times(2, h + 1))
                ch.link(nc.vector.tensor_tensor(shift[:, :, c], nmax[:, :, c], den[:, :, c], ALU.subtract))
                out = shp[:, c].rearrange("p i n a -> p n a i")
                ch.link(nc.vector.tensor_copy(out[:, 0], shift[:, :, c]))
                ch.link(nc.vector.tensor_tensor(rest[:, :, c], shift[:, :, c], out[:, 0], ALU.subtract))
                ch.link(nc.vector.tensor_copy(out[:, 1], rest[:, :, c]))
                ch.n += 1
                nc.vector.tensor_tensor(out[:, 2], rest[:, :, c], out[:, 1], ALU.subtract).then_inc(s_chain, 1)
                dve.wait_ge(s_chain, g.times(10, ch.n))
                dve.sem_inc(s_sh, 1)

            def shift_rows(g, name, number):
                h = halves(name)
                dve.wait_ge(s_misc, number)
                if g.past(1):
                    dve.wait_ge(s_shout[h], g.times(16))
                nc.vector.tensor_copy(shrow[:, h], miscb[0:3 * NP, 0:HALF]).then_inc(s_shrow, 1)
                dve.wait_ge(s_shrow, g.times(2, h + 1))
                dve.sem_inc(s_mread, 1)

            def maxima(u, number, slot):
                i, pair, cnt = RU[u]
                dve.wait_ge(s_slot, number)
                src = score[slot]
                if cnt == 2:
                    nc.vector.tensor_reduce(nmax[:, pair:pair + 2, i:i + 1], src[:, :, 0:(i + 1) * P], AX.X,
                                            ALU.max, negate=True).then_inc(s_max, 1)
                else:
                    nc.vector.tensor_reduce(nmax[:, pair, i:i + 1],
                                            src[:].rearrange("p a b -> p (a b)")[:, 0:(i + 1) * P], AX.X,
                                            ALU.max, negate=True).then_inc(s_max, 1)

            def output(g, h):
                dve.wait_ge(s_pv, g.times(NV, (NV // 3, NV)[h]))
                nc.vector.tensor_copy(oT[:, h * HALF:(h + 1) * HALF], acc[:]).then_inc(s_oT, 1)

            def rotate_first(w):
                if w == 0:
                    dve.wait_ge(s_turn, 16 * 2)
                v = nc.vector
                ch = Chain(dve, s_rot, first, 12)
                ch.n = 6 * w
                dve.wait_ge(s_swap, w + 1)
                v.tensor_tensor(rot[:], raw[:], cos[:], ALU.mult).then_inc(s_cosm, 1)
                ch.link(v.tensor_tensor(swapped[:], swapped[:], sin[:], ALU.mult))
                dve.wait_ge(s_cosm, w + 1)
                ch.link(v.tensor_tensor(rot[:], rot[:], swapped[:], ALU.add))
                ch.link(v.tensor_copy(pieces[:, w, 0], rot[:]))
                ch.link(v.tensor_tensor(rot[:], rot[:], pieces[:, w, 0], ALU.subtract))
                ch.link(v.tensor_copy(pieces[:, w, 1], rot[:]))
                ch.link(v.tensor_tensor(pieces[:, w, 2], rot[:], pieces[:, w, 1], ALU.subtract))

            for w in range(2):
                for name in PROJECT[2 * w:2 * w + 2]:
                    project(first, name, use0(0, name))
                rotate_first(w)
            dve.wait_ge(s_const, 16 * 10)
            nc.vector.tensor_tensor(lam_p[:, 0], lam_in[:, 0], lam_in[:, 1], ALU.mult).then_inc(s_lam, 1)
            nc.vector.tensor_tensor(lam_p[:, 1], lam_in[:, 2], lam_in[:, 3], ALU.mult).then_inc(s_lam, 1)
            dve.wait_ge(s_lam, 2)
            nc.vector.tensor_reduce(lam_e[:], lam_p[:], AX.X, ALU.add).then_inc(s_lam, 1)
            dve.wait_ge(s_lam, 4)
            nc.vector.tensor_tensor(nlam[:], lam_e[:, 1], lam_e[:, 0], ALU.subtract).then_inc(s_lam, 1)
            dve.wait_ge(s_lam, 5)
            nc.vector.tensor_scalar(nlam[:], nlam[:], LAMBDA_INIT, None, ALU.subtract).then_inc(s_lam, 1)

            for name in PROJECT[:2]:
                project(second, name, use0(1, name))
            for n in range(FIRST):
                maxima(n, n + 1, n % NSLOT)
            shift_pieces(first, 0)
            shift_rows(first, "shift0", use0(0, "shift0"))
            for name in PROJECT[2:]:
                project(second, name, use0(1, name))

            def body(g):
                for kind, u, n in step_events(g):
                    if kind in ("rows", "ahead"):
                        maxima(u, count(g, n), (FIRST + n) % NSLOT)
                    elif kind == "sums":
                        shift_pieces(g if u else g.back(-1), u)
                    elif kind == "out":
                        output(g.back(1) if u else g, u)
                    elif kind == "use" and u in PROJECT:
                        project(g.back(-2), u, use_in(g, u))
                    elif kind == "use" and u in LOWPASS:
                        lowpass(g.back(1), u, use_in(g, u))
                    elif kind == "use":
                        shift_rows(g.back(-1) if u == "shift0" else g, u, use_in(g, u))
            group_steps(dve, body)
            g = Step(None, NG - 1, 2)
            output(g, 1)
            for name in LOWPASS:
                lowpass(g, name, final_use(name))
                h = halves(name)
                cols = slice(h * HALF, (h + 1) * HALF)
                if name == "low0":
                    dve.wait_ge(s_att, g.times(2))
                if name[0] == "l":
                    nc.vector.tensor_tensor(sq[:, cols], y[:, cols], y[:, cols], ALU.mult).then_inc(s_sq, 1)
            for h in range(2):
                cols = slice(h * HALF, (h + 1) * HALF)
                ch = Chain(dve, s_newton, g, 8)
                ch.n = 4 * h
                dve.wait_ge(s_rs, g.times(4, 2 * h + 2))
                dve.wait_ge(s_mread, final_use(f"square{h}"))
                ch.link(nc.vector.tensor_tensor(newton[:], rs[:], rs[:], ALU.mult))
                ch.link(nc.vector.tensor_tensor(newton[:], newton[:], sq[:, cols], ALU.mult))
                ch.link(nc.vector.tensor_scalar(newton[:], newton[:], -0.5, 1.5, ALU.mult, ALU.add))
                ch.link(nc.vector.tensor_tensor(newton[:], newton[:], rs[:], ALU.mult))
                nc.vector.tensor_tensor(y[:, cols], y[:, cols], newton[:], ALU.mult).then_inc(s_att, 1)
                dve.wait_ge(s_att, g.times(2, h + 1))

        @block.scalar
        def _(act):
            nc.scalar.preload_act_table_set("natural_log_exp_and_others")
            act.wait_ge(s_lam, 3)
            nc.scalar.activation(lam_e[:], lam_e[:], ACT.Exp).then_inc(s_lam, 1)

            def log(g, h):
                c = slice(h * SH, (h + 1) * SH)
                if h:
                    act.wait_ge(s_exp, count(g, place_of(g, "rows", NU - 1)))
                elif g.past(1) or g.reg is not None:
                    act.wait_ge(s_exp, count(g.back(1), place["ahead", FIRST - 1]))
                else:
                    act.wait_ge(s_exp, FIRST)
                nc.scalar.activation(den[:, :, c], den[:, :, c], ACT.Ln).then_inc(s_ln, 1)

            def root(g, h, number):
                act.wait_ge(s_mread, number)
                if h or g.past(1):
                    act.wait_ge(s_newton, g.times(8, 4 * h))
                nc.scalar.activation(rs[:], sq[:, h * HALF:(h + 1) * HALF], ACT.Ln).then_inc(s_rs, 1)
                act.wait_ge(s_rs, g.times(4, 2 * h + 1))
                nc.scalar.activation(rs[:], rs[:], ACT.Exp, scale=-0.5).then_inc(s_rs, 1)

            def sums(u, maxed, slot):
                i, pair, cnt = RU[u]
                act.wait_ge(s_max, maxed)
                src = score[slot]
                for k in range(cnt):
                    s = src[:, k, 0:(i + 1) * P] if cnt == 2 else src[:].rearrange("p a b -> p (a b)")[:, 0:(i + 1) * P]
                    ins = nc.scalar.activation(s, s, ACT.Exp, bias=nmax[:, pair + k, i:i + 1],
                                               accum_out=den[:, pair + k, i:i + 1])
                ins.then_inc(s_exp, 1)

            for n in range(FIRST):
                sums(n, n + 1, n % NSLOT)
            log(first, 0)

            def body(g):
                done = FIRST
                for kind, u, n in step_events(g):
                    number, slot = count(g, n), (FIRST + n) % NSLOT
                    if kind in ("rows", "ahead"):
                        if u == FIRST and g.past(1):
                            act.wait_ge(s_chain, g.times(10))
                        if (kind, u) == ("ahead", 0):
                            act.wait_ge(s_chain, g.times(10, 5))
                        done += 1
                        sums(u, g.times(NU, done), slot)
                    elif kind == "root":
                        root(g.back(1), u, use_in(g, f"square{u}"))
                    elif kind == "sums":
                        log(g if u else g.back(-1), u)
                    elif kind == "probs":
                        h, j, which, head = PU[u]
                        act.wait_ge(s_slot, number)
                        if g.reg is not None or g.c * NQ + u >= NPROB:
                            act.wait_ge(s_pv, g.times(NV, (u - NPROB) // 2 + 1))
                        t0 = max(j * P - h * HALF, 0)
                        nc.scalar.activation(prob[:, u % NPROB, :, t0:HALF], score[slot][:, :, t0:HALF],
                                             ACT.Exp).then_inc(s_exp, 1)
            group_steps(act, body)
            for h in range(2):
                root(Step(None, NG - 1, 2), h, final_use(f"square{h}"))

        @block.gpsimd
        def _(pool):
            def scale_v(g):
                wait_alone(pool, s_vg[g.slot], g.round(16, 16), mark_pool)
                if not g.past(1):
                    pool.wait_ge(s_lam, 6)
                if g.past(2):
                    wait_alone(pool, s_pv, g.times(NV, -NV), mark_pool)
                nc.gpsimd.tensor_scalar(vn[:, g.slot], vg[:, g.slot], nlam[:], None, ALU.mult).then_inc(s_vn, 1)

            def rotate(g, w):
                ch = Chain(pool, s_rot, g, 12, mark_pool)
                ch.n = 6 * w
                wait_alone(pool, s_swap, g.times(2, w + 1), mark_pool)
                nc.gpsimd.tensor_tensor(rot[:], raw[:], cos[:], ALU.mult).then_inc(s_cosm, 1)
                ch.link(nc.gpsimd.tensor_tensor(swapped[:], swapped[:], sin[:], ALU.mult))
                wait_alone(pool, s_cosm, g.times(2, w + 1), mark_pool)
                ch.link(nc.gpsimd.tensor_tensor(rot[:], rot[:], swapped[:], ALU.add))
                if g.past(1):
                    wait_alone(pool, s_piece[w], g.times(16), mark_pool)
                ch.link(nc.gpsimd.tensor_copy(pieces[:, w, 0], rot[:]))
                ch.link(nc.gpsimd.tensor_tensor(rot[:], rot[:], pieces[:, w, 0], ALU.subtract))
                ch.link(nc.gpsimd.tensor_copy(pieces[:, w, 1], rot[:]))
                ch.link(nc.gpsimd.tensor_tensor(pieces[:, w, 2], rot[:], pieces[:, w, 1], ALU.subtract))
                pieces_out(g, w)

            def pieces_out(g, w):
                if g.past(2):
                    wait_alone(pool, s_stack[w][g.slot], g.round(96), mark_pool)
                pool.dma_start(piece_scr[g.slot, w].rearrange("p r t -> r p t"), pieces[:, w]).then_inc(s_piece[w], 16)

            def squares(g, h):
                cols = slice(h * HALF, (h + 1) * HALF)
                wait_alone(pool, s_y, g.times(2, h + 1), mark_pool)
                if g.past(1):
                    wait_alone(pool, s_att, g.times(2, h - 1), mark_pool)
                nc.gpsimd.tensor_tensor(sq[:, cols], y[:, cols], y[:, cols], ALU.mult).then_inc(s_sq, 1)

            def normalised(g, h):
                cols = slice(h * HALF, (h + 1) * HALF)
                ch = Chain(pool, s_newton, g, 8, mark_pool)
                ch.n = 4 * h
                wait_alone(pool, s_rs, g.times(4, 2 * h + 2), mark_pool)
                ch.link(nc.gpsimd.tensor_tensor(newton[:], rs[:], rs[:], ALU.mult))
                ch.link(nc.gpsimd.tensor_tensor(newton[:], newton[:], sq[:, cols], ALU.mult))
                ch.link(nc.gpsimd.tensor_scalar(newton[:], newton[:], -0.5, 1.5, ALU.mult, ALU.add))
                ch.link(nc.gpsimd.tensor_tensor(newton[:], newton[:], rs[:], ALU.mult))
                nc.gpsimd.tensor_tensor(y[:, cols], y[:, cols], newton[:], ALU.mult).then_inc(s_att, 1)
                wait_alone(pool, s_att, g.times(2, h + 1), mark_pool)

            nc.gpsimd.memset(kst[PIECES:ROWS + 29, 0:2], 1.0).then_inc(s_ones, 1)
            pool.wait_ge(s_ones, 1)
            for w in range(2):
                pool.wait_ge(s_rot, 6 * (w + 1))
                pieces_out(first, w)
            pool.wait_ge(s_turn, 16 * 2)
            scale_v(first)
            rotate(second, 0)

            def body(g):
                if is_more(g, 1):
                    rotate(g.back(-1), 1)
                if g.past(1):
                    for h in range(2):
                        squares(g.back(1), h)
                if is_more(g, 1):
                    scale_v(g.back(-1))
                if g.past(1):
                    for h in range(2):
                        normalised(g.back(1), h)
                if is_more(g, 2):
                    rotate(g.back(-2), 0)
            group_steps(pool, body)



R = 4
NH = NX * IX
NHL = NH + NX


class Experts:

    def __init__(self, nc, ctx, pre, w, mark_pool, mark_dve):
        def sb(name, shape, dt=F32):
            return ctx.enter_context(nc.sbuf_tensor(pre + name, shape, dt))

        def sem(name):
            return ctx.enter_context(nc.semaphore(pre + name))
        self.mark_pool, self.mark_dve = mark_pool, mark_dve
        self.nc, self.w = nc, w
        self.x, self.n1, self.x2 = sb("x", [P, R, E]), sb("n1", [P, 2, E]), sb("x2", [P, R, E])
        self.n1T = sb("n1T", [P, 2, E])
        self.st, self.mv, self.rstd = sb("st", [P, R, 6]), sb("mv", [P, R, 2]), sb("rstd", [P, R, 1])
        self.half = sb("half", [P, 1])
        self.e, self.top, self.we = sb("e", [P, 2, NH]), sb("top", [P, 2, 1]), sb("we", [P, 2, NX])
        self.tot = sb("tot", [P, 2, 1])
        self.gt, self.eq = sb("gt", [P, NX, NX]), sb("eq", [P, NX, NX])
        self.rank, self.gate = sb("rank", [P, NX]), sb("gate", [P, NX])
        self.ga, self.gaT = sb("ga", [P, 2, NH]), sb("gaT", [P, 2, P])
        self.s_x, self.s_stat, self.s_var, self.s_rstd = sem("s_x"), sem("s_stat"), sem("s_var"), sem("s_rstd")
        self.s_half, self.s_n1, self.s_t1, self.s_n1T = sem("s_half"), sem("s_n1"), sem("s_t1"), sem("s_n1T")
        self.s_h, self.s_top, self.s_e, self.s_gate = sem("s_h"), sem("s_top"), sem("s_e"), sem("s_gate")
        self.s_ga, self.s_tg, self.s_gaT, self.s_u, self.s_x2 = (sem(n) for n in ("s_ga", "s_tg", "s_gaT", "s_u",
                                                                                 "s_x2"))

    def dve_stats(self, dve, t):
        dve.wait_ge(self.s_x, t.times(1, 1))
        self.nc.vector.bn_stats(self.st[:, t.slot], self.x[:, t.slot]).then_inc(self.s_stat, 1)
        wait_alone(dve, self.s_stat, t.times(2, 1), self.mark_dve)
        self.nc.vector.bn_aggr(self.mv[:, t.slot], self.st[:, t.slot]).then_inc(self.s_stat, 1)

    def dve_norm(self, dve, t):
        dve.wait_ge(self.s_rstd, t.times(1, 1))
        if t.past(2):
            dve.wait_ge(self.s_t1, t.times(1, -1))
        self.nc.vector.tensor_scalar(self.n1[:, t.c % 2], self.x[:, t.slot], self.mv[:, t.slot, 0:1],
                                     self.rstd[:, t.slot], ALU.subtract, ALU.mult).then_inc(self.s_n1, 1)

    def dve_top(self, dve, t, hl):
        dve.wait_ge(self.s_h, t.times(1, 1))
        if t.past(2):
            dve.wait_ge(self.s_e, t.times(2, -2))
        self.nc.vector.tensor_reduce(self.top[:, t.c % 2], hl[:, NH:NHL], AX.X, ALU.max, negate=True)\
            .then_inc(self.s_top, 1)

    def dve_gate(self, dve, t, hl):
        v, k = self.nc.vector, t.c % 2
        ch = Chain(dve, self.s_gate, t, 11)
        dve.wait_ge(self.s_e, t.times(2, 2))
        we = self.we[:, k]
        other = we.rearrange("p (o e) -> p o e", o=1).broadcast_to([P, NX, NX])
        own = we.rearrange("p (e o) -> p e o", o=1).broadcast_to([P, NX, NX])
        ch.beside(v.tensor_tensor(self.eq[:], other, own, ALU.is_equal))
        ch.beside(v.tensor_tensor(self.gt[:], other, own, ALU.is_gt))
        ch.beside(v.reciprocal(self.tot[:, k], self.tot[:, k]))
        ch.link(v.tensor_scalar(self.e[:, k], self.e[:, k], 1.0, None, ALU.add))
        ch.beside(v.tensor_tensor(self.eq[:], self.eq[:], self.w["tri"][:], ALU.mult))
        ch.link(v.reciprocal(self.e[:, k], self.e[:, k]))
        ch.beside(v.tensor_tensor(self.e[:, k], self.e[:, k], hl[:, 0:NH], ALU.mult))
        ch.link(v.tensor_tensor(self.gt[:], self.gt[:], self.eq[:], ALU.add))
        ch.link(v.tensor_reduce(self.rank[:], self.gt[:], AX.X, ALU.add))
        ch.link(v.scalar_tensor_tensor(self.gate[:], self.rank[:], 1.5, we, ALU.is_lt, ALU.mult))
        ch.link(v.tensor_scalar(self.gate[:], self.gate[:], self.tot[:, k], None, ALU.mult))
        ch.end()
        if t.past(2):
            dve.wait_ge(self.s_tg, t.times(1, -1))
        v.tensor_tensor(self.ga[:, k].rearrange("p (e i) -> p e i", e=NX),
                        self.e[:, k].rearrange("p (e i) -> p e i", e=NX),
                        self.gate[:].rearrange("p (e o) -> p e o", o=1).broadcast_to([P, NX, IX]), ALU.mult)\
            .then_inc(self.s_ga, 1)
        dve.wait_ge(self.s_ga, t.times(1, 1))

    def dve_sum(self, dve, t, bank):
        dve.wait_ge(self.s_u, t.times(1, 1))
        self.nc.vector.tensor_tensor(self.x2[:, t.slot], bank[:], self.x[:, t.slot], ALU.add).then_inc(self.s_x2, 1)

    def pool_start(self, pool):
        self.nc.gpsimd.memset(self.half[:], -0.5).then_inc(self.s_half, 1)
        pool.wait_ge(self.s_half, 1)

    def pool_rstd(self, pool, t):
        g = self.nc.gpsimd
        wait_alone(pool, self.s_stat, t.times(2, 2), self.mark_pool)
        if t.past(R):
            wait_alone(pool, self.s_n1, t.times(1, 1 - R), self.mark_pool)
        g.tensor_scalar(self.rstd[:, t.slot], self.mv[:, t.slot, 1:2], EPS, None, ALU.add).then_inc(self.s_var, 1)
        wait_alone(pool, self.s_var, t.times(1, 1), self.mark_pool)
        g.tensor_tensor(self.rstd[:, t.slot], self.rstd[:, t.slot], self.half[:], ALU.pow).then_inc(self.s_rstd, 1)

    def act_n1T(self, act, t, bank):
        act.wait_ge(self.s_t1, t.times(1, 1))
        if t.past(2):
            act.wait_ge(self.s_h, t.times(1, -1))
        self.nc.scalar.copy(self.n1T[:, t.c % 2], bank[:]).then_inc(self.s_n1T, 1)

    def act_exps(self, act, t, hl):
        k = t.c % 2
        act.wait_ge(self.s_top, t.times(1, 1))
        if t.past(2):
            act.wait_ge(self.s_ga, t.times(1, -1))
        self.nc.scalar.activation(self.e[:, k], hl[:, 0:NH], ACT.Exp, scale=-1.0).then_inc(self.s_e, 1)
        self.nc.scalar.activation(self.we[:, k], hl[:, NH:NHL], ACT.Exp, bias=self.top[:, k],
                                  accum_out=self.tot[:, k]).then_inc(self.s_e, 1)

    def act_gaT(self, act, t, bank):
        act.wait_ge(self.s_tg, t.times(1, 1))
        if t.past(2):
            act.wait_ge(self.s_u, t.times(1, -1))
        self.nc.scalar.copy(self.gaT[:, t.c % 2], bank[:, 0:P]).then_inc(self.s_gaT, 1)

    def pe_turn(self, pe, t, bank):
        pe.wait_ge(self.s_n1, t.times(1, 1))
        for c in range(KC):
            mm = self.nc.tensor.transpose(bank[:, c * P:(c + 1) * P], self.n1[:, t.c % 2, c * P:(c + 1) * P],
                                          self.w["ident"][:])
        mm.then_inc(self.s_t1, 1)

    def pe_down(self, pe, t, hl):
        pe.wait_ge(self.s_n1T, t.times(1, 1))
        if t.past(1):
            pe.wait_ge(self.s_ga, t.times(1))
        for c in range(KC):
            mm = self.nc.tensor.matmul(hl[:, 0:NHL], self.n1T[:, t.c % 2, c * P:(c + 1) * P], self.w["down"][:, c],
                                       start=(c == 0), stop=(c == KC - 1))
        mm.then_inc(self.s_h, 1)

    def pe_turn_ga(self, pe, t, bank):
        pe.wait_ge(self.s_ga, t.times(1, 1))
        self.nc.tensor.transpose(bank[:, 0:P], self.ga[:, t.c % 2], self.w["ident"][:]).then_inc(self.s_tg, 1)

    def pe_up(self, pe, t, bank):
        pe.wait_ge(self.s_gaT, t.times(1, 1))
        if t.past(1):
            pe.wait_ge(self.s_x2, t.times(1))
        self.nc.tensor.matmul(bank[:], self.gaT[:, t.c % 2], self.w["up"][:], start=True, stop=True)\
            .then_inc(self.s_u, 1)



def middle(nc, marks, a, x_tiles, att_scr, qt_scr, res_scr, w):
    with ExitStack() as ctx:
        def sb(name, shape, dt=F32):
            return ctx.enter_context(nc.sbuf_tensor("m_" + name, shape, dt))

        def sem(name):
            return ctx.enter_context(nc.semaphore("m_" + name))
        mark_sp, mark_pool, mark_dve = marks

        def bank(name):
            return ctx.enter_context(nc.psum_tensor("m_" + name, [P, E], F32))
        ident, wab, bout = w["ident"], w["wab"], w["bout"]
        ex = Experts(nc, ctx, "m_", w, mark_pool, mark_dve)
        rms, lnw, lnb = w["rms"], w["lnw"], w["lnb"]
        lnbb = sb("lnbb", [P, KC, P])
        bin_ = sb("bin", [P, 3 * E])
        win, wo, wout, res = w["win"], w["wo"], w["wout"], w["res"]
        which = sb("which", [P, NT, B])
        woh, wol = sb("woh", [P, KC, E], F32R), sb("wol", [P, KC, E], F32R)
        winh, winl = sb("winh", [P, KC, 3 * E], F32R), sb("winl", [P, KC, 3 * E], F32R)
        aT = sb("aT", [P, 2, KC, P])
        aTh, aTl = sb("aTh", [P, 2, KC, P], F32R), sb("aTl", [P, 2, KC, P], F32R)
        xin = sb("xin", [P, 2, E])
        rope = sb("rope", [P, 2, 2, NROPE])
        st2, mv2 = sb("st2", [P, R, 6]), sb("mv2", [P, R, 2])
        r1, v2, r12 = sb("r1", [P, R, 1]), sb("v2", [P, R, 1]), sb("r12", [P, R, 1])
        n2, h2 = sb("n2", [P, 2, E]), sb("h2", [P, 2, E])
        hTh, hTl = sb("hTh", [P, 2, E], F32R), sb("hTl", [P, 2, E], F32R)
        q, k, v = sb("q", [P, 2, E]), sb("k", [P, 2, E]), sb("v", [P, 2, E])
        sw, sq = sb("sw", [P, NROPE]), sb("sq", [P, E])
        ss, rinv = sb("ss", [P, 2, 1]), sb("rinv", [P, 2, 1])
        wr = sb("wr", [P, 2, B])
        qT = sb("qT", [P, 2, KC, P])
        arow = sb("arow", [B, E])
        acol = sb("acol", [P, KC, B])

        t0, t1, hl, bw, bu, b0, b1, ba = (bank(n) for n in ("t0", "t1", "hl", "bw", "bu", "b0", "b1", "ba"))
        s_const, s_constb, s_prep, s_bias, s_fold = (sem(n) for n in ("const", "constb", "prep", "bias", "fold"))
        s_in = [sem(f"in{i}") for i in range(2)]
        s_aTh, s_aTl, s_hTl, s_wh, s_wl = (sem(n) for n in ("aTh", "aTl", "hTl", "wh", "wl"))
        s_wout = sem("wout_in")
        s_w, s_st2, s_rr, s_n2, s_h2 = sem("w"), sem("st2"), sem("rr"), sem("n2"), sem("h2")
        s_t2, s_hT, s_q, s_k, s_v, s_kb, s_vb, s_qb = (sem(n) for n in ("t2", "hT", "q", "k", "v", "kb", "vb", "qb"))
        s_ss, s_rope, s_kv, s_qr, s_wr, s_acc, s_tq, s_qT = (sem(n) for n in ("ss", "rope", "kv", "qr", "wr", "acc",
                                                                             "tq", "qT"))
        s_res, s_tail, s_fold2, s_ropein, s_wrc, s_rrc = (sem(n) for n in ("res", "tail", "fold2", "ropein", "wrc",
                                                                          "rrc"))
        s_resd = [sem(f"resd{i}") for i in range(R)]
        s_qTd = [sem(f"qTd{i}") for i in range(2)]
        NCONST, NCONSTB = 4, 3
        block = ctx.enter_context(nc.Block())

        def modulo(eng, t):
            return t.c % TB if t.reg is None else eng.snap(t.times(1)) % TB

        def batch(eng, t):
            return t.c // TB if t.reg is None else eng.snap(t.times(1)) // TB

        def by2(t, per, add=0):
            if t.reg is None:
                return (t.c // 2) * per + add
            return t.reg * (t.stride // 2 * per) + ((t.c // 2) * per + add)

        @block.sync
        def _(sp):
            def load_tile(t):
                if t.past(2):
                    wait_alone(sp, ex.s_x, t.times(1, -1), mark_sp)
                time = modulo(sp, t)
                b4 = batch(sp, t) * G
                k_ = t.c % 2
                sp.dma_start(aT[:, k_], att_scr[bass.ds(b4, G), :, bass.ds(time * P, P)]
                             .rearrange("g p t -> p g t")).then_inc(s_in[k_], 16)
                sp.dma_start(xin[:, k_], x_tiles[bass.ds(t.times(1), 1)].rearrange("a p e -> p (a e)"))\
                    .then_inc(s_in[k_], 16)

            consts = [
                      (w["down"][:, :, 0:NH], a["down_w"].rearrange("(c p) e i -> p c (e i)", p=P)),
                      (w["down"][:, :, NH:NHL], a["router_w"].rearrange("(c p) e -> p c e", p=P)),
                      (w["tri"][:], a["c_tri"].rearrange("p (e f) -> p e f", e=NX)),
                      (w["up"][:], a["up_w"].rearrange("e i h -> (e i) h"))]
            later = [(bout[:], a["b_out"].rearrange("(o n) -> o n", o=1).broadcast_to([P, E])),
                     (which[:], a["c_which"].rearrange("p (t b) -> p t b", b=B)),
                     (bin_[:], a["b_in"].rearrange("(o n) -> o n", o=1).broadcast_to([P, 3 * E]))]
            assert (len(consts), len(later)) == (NCONST, NCONSTB)
            load_tile(Step(None, 0, R))
            for dst, src in consts:
                sp.dma_start(dst, src, allow_slow_non_contiguous=True).then_inc(s_const, 16)
            load_tile(Step(None, 1, R))
            for dst, src in later:
                sp.dma_start(dst, src, allow_slow_non_contiguous=True).then_inc(s_constb, 16)
            load_tile(Step(None, 2, R))
            load_tile(Step(None, 3, R))

            sp.wait_ge(s_wl, 2 * KC)
            sp.dma_start(wout, a["W_out"].rearrange("(c p) n -> p c n", p=P)).then_inc(s_wout, 16)

            def body(t):
                if t.reg is not None or t.c >= 4:
                    load_tile(t)
            steps(sp, NT, R, 2 * R, NT, body)

        @block.tensor
        def _(pe):
            mmul = nc.tensor.matmul

            def product(b, xh, xl, wh, wl, col):
                for c in range(KC):
                    for n, (x, y) in enumerate(((xh, wh), (xl, wh), (xh, wl))):
                        mm = mmul(b[:], x[:, c * P:(c + 1) * P], y[:, c, col:col + E], start=(c == 0 and n == 0),
                                  stop=(c == KC - 1 and n == 2))
                return mm
            pe.wait_ge(s_prep, 1)
            for c in range(KC):
                for n, b in enumerate((b0, b1, ba)):
                    mm = mmul(b[:], lnbb[:, c], win[c][:, n * E:(n + 1) * E], start=(c == 0),
                              stop=(c == KC - 1))
                mm.then_inc(s_bias, 1)
            pe.wait_ge(s_const, 16 * NCONST)
            pe.wait_ge(s_wl, KC)

            def project(t, b, part, done):
                product(b, hTh[:, t.c % 2], hTl[:, t.c % 2], winh, winl, part * E).then_inc(done, 1)

            def body(s):
                t = s.back(1)
                if t.exists(NT):
                    if t.past(4):
                        pe.wait_ge(s_qT, t.times(1, -3))
                    ex.pe_turn(pe, t, t0)
                t = s.back(2)
                if t.exists(NT):
                    if t.past(2):
                        pe.wait_ge(s_hTl, t.times(1, -1))
                    ex.pe_turn_ga(pe, t, t1)
                t = s.back(1)
                if t.exists(NT):
                    ex.pe_down(pe, t, hl)
                t = s.back(3)
                if t.exists(NT):
                    pe.wait_ge(s_h2, t.times(1, 1))
                    pe.wait_ge(ex.s_gaT, s.back(2).times(1, 1) if s.back(2).exists(NT) else NT)
                    if t.past(1) and not s.back(2).exists(NT):
                        pe.wait_ge(s_hTl, t.times(1))
                    for c in range(KC):
                        mm = nc.tensor.transpose(t1[:, c * P:(c + 1) * P], h2[:, t.c % 2, c * P:(c + 1) * P], ident[:])
                    mm.then_inc(s_t2, 1)
                t = s
                if t.exists(NT):
                    pe.wait_ge(s_aTl, t.times(1, 1))
                    if t.past(1):
                        pe.wait_ge(ex.s_x, t.times(1))
                    product(bw, aTh[:, t.c % 2].rearrange("p c t -> p (c t)"),
                            aTl[:, t.c % 2].rearrange("p c t -> p (c t)"), woh, wol, 0).then_inc(s_w, 1)
                t = s.back(2)
                if t.exists(NT):
                    ex.pe_up(pe, t, bu)
                if s.reg is None and s.c == 3:
                    pe.wait_ge(s_fold2, 3 + KC)
                    pe.wait_ge(s_wl, 2 * KC)
                t = s.back(3)
                if t.exists(NT):
                    pe.wait_ge(s_hTl, t.times(1, 1))
                    for n, (b, done) in enumerate(((b0, s_k), (b1, s_v))):
                        if t.past(1):
                            pe.wait_ge((s_qb, s_vb)[n], t.times(1))
                        project(t, b, 1 + n, done)
                t = s.back(4)
                if t.exists(NT):
                    pe.wait_ge(s_qr, t.times(1, 1))
                    pe.wait_ge(ex.s_n1T, s.back(1).times(1, 1) if s.back(1).exists(NT) else NT)
                    if t.past(1) and not s.back(1).exists(NT):
                        pe.wait_ge(s_qT, t.times(1))
                    for c in range(KC):
                        mm = nc.tensor.transpose(t0[:, c * P:(c + 1) * P], q[:, t.c % 2, c * P:(c + 1) * P], ident[:])
                    mm.then_inc(s_tq, 1)
                t = s.back(4)
                if t.exists(NT):
                    pe.wait_ge(s_kv, t.times(1, 1))
                    pe.wait_ge(s_wr, t.times(1, 1))
                    one = t.reg is None
                    mmul(ba[0:B, :], wr[:, t.c % 2], k[:, t.c % 2], start=(one and t.c == 0),
                         stop=(one and t.c == NT - 1)).then_inc(s_acc, 1)
                t = s.back(3)
                if t.exists(NT):
                    pe.wait_ge(s_kb, t.times(1, 1))
                    project(t, b0, 0, s_q)
            steps(pe, NT, R, 2 * R, NT + 4, body)
            pe.wait_ge(s_tail, 1)
            for c in range(KC):
                mm = nc.tensor.transpose(t1[:, c * B:(c + 1) * B], arow[:, c * P:(c + 1) * P], ident[0:B, 0:B])
            mm.then_inc(s_tail, 1)

        @block.vector
        def _(dve):
            vec = nc.vector
            vec.tensor_copy(lnbb[:], lnb[:].rearrange("p (c o) -> p c o", o=1).broadcast_to([P, KC, P]))\
                .then_inc(s_prep, 1)
            for c in range(KC):
                vec.tensor_scalar(wo[:, c], wo[:, c], rms[:], 1.0 - LAMBDA_INIT, ALU.mult, ALU.mult)\
                    .then_inc(s_fold, 1)
            for c in range(KC):
                dve.wait_ge(s_wh, c + 1)
                vec.tensor_tensor(wol[:, c], wo[:, c], woh[:, c].bitcast(F32), ALU.subtract).then_inc(s_wl, 1)

            def rest_a(t):
                dve.wait_ge(s_aTh, t.times(1, 1))
                if t.past(2):
                    dve.wait_ge(s_w, t.times(1, -1))
                vec.tensor_tensor(aTl[:, t.c % 2], aT[:, t.c % 2], aTh[:, t.c % 2].bitcast(F32), ALU.subtract)\
                    .then_inc(s_aTl, 1)

            for c in range(KC + 1):
                if c == 2:
                    rest_a(Step(None, 0, R))
                if c < KC:
                    dve.wait_ge(s_bias, c + 1)
                    vec.tensor_scalar(win[c], win[c], lnw[:, c:c + 1], None, ALU.mult).then_inc(s_fold2, 1)
                if c > 0:
                    dve.wait_ge(s_wh, KC + c)
                    vec.tensor_tensor(winl[:, c - 1], win[c - 1], winh[:, c - 1].bitcast(F32), ALU.subtract)\
                        .then_inc(s_wl, 1)
            dve.wait_ge(s_const, 16 * NCONST)

            def body(s):
                t = s
                if t.exists(NT) and (t.reg is not None or t.c > 0):
                    rest_a(t)
                t = s.back(1)
                if t.exists(NT):
                    ex.dve_top(dve, t, hl)
                t = s.back(3)
                if t.exists(NT):
                    dve.wait_ge(s_hT, t.times(1, 1))
                    if t.past(2):
                        dve.wait_ge(s_q, t.times(1, -1))
                    vec.tensor_tensor(hTl[:, t.c % 2], t1[:], hTh[:, t.c % 2].bitcast(F32), ALU.subtract)\
                        .then_inc(s_hTl, 1)
                t = s.back(4)
                if t.exists(NT):
                    i = t.c % 2
                    dve.wait_ge(s_rope, t.times(8, 4))
                    dve.wait_ge(s_ss, t.times(1, 1))
                    dve.wait_ge(s_vb, t.times(1, 1))
                    vec.tensor_tensor(k[:, i], k[:, i], v[:, i], ALU.mult).then_inc(s_kv, 1)
                t = s
                if t.exists(NT):
                    dve.wait_ge(s_w, t.times(1, 1))
                    if t.past(R):
                        dve.wait_ge(ex.s_x2, t.times(1, 1 - R))
                    vec.tensor_tensor(ex.x[:, t.slot], bw[:], xin[:, t.c % 2], ALU.add).then_inc(ex.s_x, 1)
                    ex.dve_stats(dve, t)
                t = s.back(2)
                if t.exists(NT):
                    ex.dve_sum(dve, t, bu)
                    dve.wait_ge(ex.s_x2, t.times(1, 1))
                    vec.bn_stats(st2[:, t.slot], ex.x2[:, t.slot]).then_inc(s_st2, 1)
                    wait_alone(dve, s_st2, t.times(2, 1), mark_dve)
                    vec.bn_aggr(mv2[:, t.slot], st2[:, t.slot]).then_inc(s_st2, 1)
                t = s.back(3)
                if t.exists(NT):
                    i = t.c % 2
                    dve.wait_ge(s_k, t.times(1, 1))
                    if t.reg is None and t.c == 0:
                        dve.wait_ge(s_fold2, 3 + KC)
                    if t.past(2):
                        dve.wait_ge(s_acc, t.times(1, -1))
                    vec.tensor_tensor(k[:, i], b0[:], bin_[:, E:2 * E], ALU.add).then_inc(s_kb, 1)
                    dve.wait_ge(s_v, t.times(1, 1))
                    vec.tensor_tensor(v[:, i], b1[:], bin_[:, 2 * E:3 * E], ALU.add).then_inc(s_vb, 1)
                t = s.back(1)
                if t.exists(NT):
                    ex.dve_gate(dve, t, hl)
                t = s
                if t.exists(NT):
                    ex.dve_norm(dve, t)
                t = s.back(2)
                if t.exists(NT):
                    dve.wait_ge(s_rr, t.times(5, 5))
                    if t.past(2):
                        dve.wait_ge(s_res, t.times(2, -2))
                        dve.wait_ge(s_t2, t.times(1, -1))
                    vec.tensor_scalar(n2[:, t.c % 2], ex.x2[:, t.slot], mv2[:, t.slot, 0:1], r1[:, t.slot],
                                      ALU.subtract, ALU.mult).then_inc(s_n2, 1)
                    vec.tensor_scalar(h2[:, t.c % 2], ex.x2[:, t.slot], mv2[:, t.slot, 0:1], r12[:, t.slot],
                                      ALU.subtract, ALU.mult).then_inc(s_h2, 1)
                t = s.back(3)
                if t.exists(NT):
                    i = t.c % 2
                    dve.wait_ge(s_q, t.times(1, 1))
                    if t.past(2):
                        dve.wait_ge(s_tq, t.times(1, -1))
                    vec.tensor_tensor(q[:, i], b0[:], bin_[:, 0:E], ALU.add).then_inc(s_qb, 1)
                if s.reg is None and s.c == 0:
                    dve.wait_ge(s_constb, 16 * NCONSTB)
                    for n, b in enumerate((b0, b1, ba)):
                        vec.tensor_tensor(bin_[:, n * E:(n + 1) * E], bin_[:, n * E:(n + 1) * E], b[:], ALU.add)\
                            .then_inc(s_fold2, 1)
            steps(dve, NT, R, 2 * R, NT + 4, body)
            dve.wait_ge(s_acc, NT)
            vec.tensor_copy(arow[:], ba[0:B, :]).then_inc(s_tail, 1)
            dve.wait_ge(s_tail, 2)
            vec.tensor_copy(acol[:], t1[:, 0:KC * B].rearrange("p (c b) -> p c b", b=B)).then_inc(s_tail, 1)
            dve.wait_ge(s_tail, 3)
            dve.wait_ge(s_wout, 16)
            for b in range(B):
                for c in range(KC):
                    vec.tensor_scalar(wab[:, b, c], wout[:, c], acol[:, c, b:b + 1], None, ALU.mult)\
                        .then_inc(s_tail, 1)

        @block.scalar
        def _(act):
            nc.scalar.preload_act_table_set("exp_and_others")
            for c in range(KC):
                act.wait_ge(s_fold, c + 1)
                nc.scalar.copy(woh[:, c], wo[:, c]).then_inc(s_wh, 1)

            def round_a(t):
                act.wait_ge(s_in[t.c % 2], by2(t, 32, 32))
                if t.past(2):
                    act.wait_ge(s_w, t.times(1, -1))
                nc.scalar.copy(aTh[:, t.c % 2], aT[:, t.c % 2]).then_inc(s_aTh, 1)

            round_a(Step(None, 0, R))
            for c in range(KC):
                act.wait_ge(s_fold2, c + 1)
                nc.scalar.copy(winh[:, c], win[c]).then_inc(s_wh, 1)

            def body(s):
                t = s.back(1)
                if t.exists(NT):
                    ex.act_n1T(act, t, t0)
                t = s
                if t.exists(NT) and (t.reg is not None or t.c > 0):
                    round_a(t)
                t = s.back(2)
                if t.exists(NT):
                    ex.act_gaT(act, t, t1)
                t = s.back(3)
                if t.exists(NT):
                    act.wait_ge(s_t2, t.times(1, 1))
                    if t.past(2):
                        act.wait_ge(s_q, t.times(1, -1))
                    nc.scalar.copy(hTh[:, t.c % 2], t1[:]).then_inc(s_hT, 1)
                t = s.back(1)
                if t.exists(NT):
                    ex.act_exps(act, t, hl)
                t = s.back(3)
                if t.exists(NT):
                    act.wait_ge(s_kb, t.times(1, 1))
                    if t.past(1):
                        act.wait_ge(s_ss, t.times(1))
                    if t.past(2):
                        act.wait_ge(s_wr, t.times(1, -1))
                    nc.scalar.activation(sq[:], k[:, t.c % 2], ACT.Square, accum_out=ss[:, t.c % 2]).then_inc(s_ss, 1)
                t = s.back(4)
                if t.exists(NT):
                    act.wait_ge(s_tq, t.times(1, 1))
                    if t.reused(2):
                        act.wait_ge(s_qTd[t.c % 2], by2(t, 16))
                    nc.scalar.copy(qT[:, t.c % 2].rearrange("p c t -> p (c t)"), t0[:]).then_inc(s_qT, 1)
                    act.wait_ge(s_qT, t.times(1, 1))
                    act.dma_start(qt_scr[bass.ds(t.times(1), 1)].rearrange("a p c t -> p (a c) t"), qT[:, t.c % 2])\
                        .then_inc(s_qTd[t.c % 2], 16)
            steps(act, NT, R, 2 * R, NT + 4, body)
            for i in range(2):
                act.wait_ge(s_qTd[i], 16 * (NT // 2))

        @block.gpsimd
        def _(pool):
            g = nc.gpsimd
            ex.pool_start(pool)

            def rotate(t, x, base):
                i = t.c % 2
                ch = Chain(pool, s_rope, t, 8, mark_pool)
                ch.n = base
                left = x[:, i, 0:NROPE]
                pairs = left.rearrange("p (n two) -> p n two", two=2)
                swp = sw[:].rearrange("p (n two) -> p n two", two=2)
                sn = rope[:, i, 1].rearrange("p (n two) -> p n two", two=2)
                ch.link(g.tensor_tensor(swp[:, :, 0], pairs[:, :, 1], sn[:, :, 0], ALU.mult))
                ch.link(g.tensor_tensor(swp[:, :, 1], pairs[:, :, 0], sn[:, :, 1], ALU.mult))
                ch.link(g.tensor_tensor(left, left, rope[:, i, 0], ALU.mult))
                ch.link(g.tensor_tensor(left, left, sw[:], ALU.add))

            def body(s):
                t = s
                if t.exists(NT):
                    ex.pool_rstd(pool, t)
                t = s.back(2)
                if t.exists(NT):
                    ch = Chain(pool, s_rr, t, 5, mark_pool)
                    wait_alone(pool, s_st2, t.times(2, 2), mark_pool)
                    if t.past(3):
                        wait_alone(pool, s_h2, t.times(1, -2), mark_pool)
                    var = mv2[:, t.slot, 1:2]
                    x1, x2, x3 = r1[:, t.slot], v2[:, t.slot], r12[:, t.slot]
                    ch.link(g.tensor_scalar(x1, var, EPS, None, ALU.add))
                    ch.link(g.tensor_tensor(x1, x1, ex.half[:], ALU.pow))
                    ch.link(g.tensor_scalar(x2, var, x1, x1, ALU.mult, ALU.mult))
                    ch.link(g.tensor_scalar(x2, x2, EPS, None, ALU.add))
                    g.tensor_tensor(x2, x2, ex.half[:], ALU.pow).then_inc(s_rrc, 1)
                    wait_alone(pool, s_rrc, t.times(1, 1), mark_pool)
                    ch.link(g.tensor_tensor(x3, x1, x2, ALU.mult))
                t = s.back(3)
                if t.exists(NT):
                    i = t.c % 2
                    pool.dma_start(rope[:, i], a["c_rope"].rearrange("(n p) (two e) -> n p two e", p=P, two=2)
                                   [bass.ds(modulo(pool, t), 1)].rearrange("n p two e -> p (n two) e"))\
                        .then_inc(s_ropein, 16)
                    wait_alone(pool, s_ropein, t.times(16, 16), mark_pool)
                    wait_alone(pool, s_ss, t.times(1, 1), mark_pool)
                    rotate(t, k, 0)
                    ch = Chain(pool, s_wrc, t, 1, mark_pool)
                    if t.past(2):
                        wait_alone(pool, s_acc, t.times(1, -1), mark_pool)
                    ch.link(g.tensor_tensor(rinv[:, i], ss[:, i], ex.half[:], ALU.pow))
                    g.tensor_tensor(wr[:, i], which[:, bass.ds(t.times(1), 1)].rearrange("p t b -> p (t b)"),
                                    rinv[:, i].broadcast_to([P, B]), ALU.mult).then_inc(s_wr, 1)
                    wait_alone(pool, s_wr, t.times(1, 1), mark_pool)
                t = s.back(2)
                if t.exists(NT):
                    wait_alone(pool, s_n2, t.times(1, 1), mark_pool)
                    if t.reused(R):
                        wait_alone(pool, s_resd[t.slot], t.round(16), mark_pool)
                    g.tensor_tensor(res[:, t.slot], ex.x2[:, t.slot], n2[:, t.c % 2], ALU.add).then_inc(s_res, 1)
                    wait_alone(pool, s_res, t.times(2, 1), mark_pool)
                    g.tensor_tensor(res[:, t.slot], res[:, t.slot], bout[:], ALU.add).then_inc(s_res, 1)
                    wait_alone(pool, s_res, t.times(2, 2), mark_pool)
                    pool.dma_start(res_scr[bass.ds(t.times(1), 1)].rearrange("a p e -> p (a e)"), res[:, t.slot])\
                        .then_inc(s_resd[t.slot], 16)
                t = s.back(3)
                if t.exists(NT):
                    wait_alone(pool, s_qb, t.times(1, 1), mark_pool)
                    rotate(t, q, 4)
                    pool.sem_inc(s_qr, 1)
            pool.wait_ge(s_constb, 16 * NCONSTB)
            pool.wait_ge(s_wl, KC)
            steps(pool, NT, R, 2 * R, NT + 4, body)
            for i in range(R):
                pool.wait_ge(s_resd[i], 16 * (NT // R))



def last(nc, marks, a, out_tiles, qt_scr, res_scr, w):
    with ExitStack() as ctx:
        def sb(name, shape, dt=F32):
            return ctx.enter_context(nc.sbuf_tensor("l_" + name, shape, dt))

        def sem(name):
            return ctx.enter_context(nc.semaphore("l_" + name))
        mark_sp, mark_pool, mark_dve = marks

        def bank(name):
            return ctx.enter_context(nc.psum_tensor("l_" + name, [P, E], F32))
        ex = Experts(nc, ctx, "l_", w, mark_pool, mark_dve)
        qT, res = sb("qT", [P, R, KC, P]), sb("res", [P, R, E])
        z = [bank("z0"), bank("z1")]
        t0, t1, hl, bu = bank("t0"), bank("t1"), bank("hl"), bank("bu")
        s_in = [sem(f"in{i}") for i in range(R)]
        s_z = sem("z")
        s_out = [sem(f"out{i}") for i in range(R)]
        block = ctx.enter_context(nc.Block())

        @block.sync
        def _(sp):
            def body(t):
                if t.past(R):
                    sp.wait_ge(ex.s_x, t.times(1, 1 - R))
                sp.dma_start(qT[:, t.slot], qt_scr[bass.ds(t.times(1), 1)].rearrange("a p c t -> p (a c) t"))\
                    .then_inc(s_in[t.slot], 16)
                sp.dma_start(res[:, t.slot], res_scr[bass.ds(t.times(1), 1)].rearrange("a p e -> p (a e)"))\
                    .then_inc(s_in[t.slot], 16)
            steps(sp, NT, R, 2 * R, NT, body)

        @block.tensor
        def _(pe):
            def body(s):
                t = s
                if t.exists(NT):
                    pe.wait_ge(s_in[t.slot], t.round(32, 32))
                    if t.past(2):
                        pe.wait_ge(ex.s_x, t.times(1, -1))
                    b = t.c // TB if t.reg is None else pe.snap(t.times(1)) // TB
                    for c in range(KC):
                        rhs = w["wab"][:, bass.ds(b, 1), c].rearrange("p b e -> p (b e)")
                        mm = nc.tensor.matmul(z[t.c % 2][:], qT[:, t.slot, c], rhs, start=(c == 0), stop=(c == KC - 1))
                    mm.then_inc(s_z, 1)
                t = s.back(1)
                if t.exists(NT):
                    if t.past(1):
                        pe.wait_ge(ex.s_n1T, t.times(1))
                    ex.pe_turn(pe, t, t0)
                t = s.back(2)
                if t.exists(NT):
                    if t.past(1):
                        pe.wait_ge(ex.s_gaT, t.times(1))
                    ex.pe_turn_ga(pe, t, t1)
                t = s.back(1)
                if t.exists(NT):
                    ex.pe_down(pe, t, hl)
                t = s.back(2)
                if t.exists(NT):
                    ex.pe_up(pe, t, bu)
            steps(pe, NT, R, 2 * R, NT + 2, body)

        @block.vector
        def _(dve):
            def body(s):
                t = s
                if t.exists(NT):
                    dve.wait_ge(s_z, t.times(1, 1))
                    if t.past(R):
                        dve.wait_ge(ex.s_x2, t.times(1, 1 - R))
                    nc.vector.tensor_tensor(ex.x[:, t.slot], z[t.c % 2][:], res[:, t.slot], ALU.add)\
                        .then_inc(ex.s_x, 1)
                    ex.dve_stats(dve, t)
                t = s.back(1)
                if t.exists(NT):
                    ex.dve_top(dve, t, hl)
                t = s.back(2)
                if t.exists(NT):
                    if t.reused(R):
                        dve.wait_ge(s_out[t.slot], t.round(16))
                    ex.dve_sum(dve, t, bu)
                t = s
                if t.exists(NT):
                    ex.dve_norm(dve, t)
                t = s.back(1)
                if t.exists(NT):
                    ex.dve_gate(dve, t, hl)
            steps(dve, NT, R, 2 * R, NT + 2, body)

        @block.scalar
        def _(act):
            def body(s):
                t = s.back(1)
                if t.exists(NT):
                    ex.act_n1T(act, t, t0)
                t = s.back(2)
                if t.exists(NT):
                    ex.act_gaT(act, t, t1)
                t = s.back(1)
                if t.exists(NT):
                    ex.act_exps(act, t, hl)
            steps(act, NT, R, 2 * R, NT + 2, body)

        @block.gpsimd
        def _(pool):
            ex.pool_start(pool)

            def body(s):
                t = s
                if t.exists(NT):
                    ex.pool_rstd(pool, t)
                t = s.back(2)
                if t.exists(NT):
                    wait_alone(pool, ex.s_x2, t.times(1, 1), mark_pool)
                    pool.dma_start(out_tiles[bass.ds(t.times(1), 1)].rearrange("a p e -> p (a e)"),
                                   ex.x2[:, t.slot]).then_inc(s_out[t.slot], 16)
            steps(pool, NT, R, 2 * R, NT + 2, body)
            for i in range(R):
                pool.wait_ge(s_out[i], 16 * (NT // R))


_SHORT = {"L0_attn_a_query": "query", "L0_attn_a_Wq": "Wq", "L0_attn_a_Wk": "Wk", "L0_attn_a_Wv": "Wv",
          "L0_attn_a_Wout": "Wout", "L0_attn_a_lambda_q1": "lambda_q1", "L0_attn_a_lambda_k1": "lambda_k1",
          "L0_attn_a_lambda_q2": "lambda_q2", "L0_attn_a_lambda_k2": "lambda_k2", "L0_attn_a_rms_weight": "rms_weight",
          "L0_attn_b_ln_w": "ln_w", "L0_attn_b_ln_b": "ln_b", "L0_attn_b_W_in": "W_in", "L0_attn_b_b_in": "b_in",
          "L0_attn_b_W_out": "W_out", "L0_attn_b_b_out": "b_out", "L0_ffn_router_w": "router_w",
          "L0_ffn_down_w": "down_w", "L0_ffn_up_w": "up_w"}


def kernel(**inputs):
    import numpy as _np
    import concourse.bacc as _bacc
    from concourse import mybir as _mybir
    from concourse.bass_utils import run_bass_kernel_spmd as _run

    nc = _bacc.Bacc("TRN2", target_bir_lowering=False, num_devices=1)
    arrays, args = {}, {}
    given = {short: inputs[name] for name, short in _SHORT.items()}
    given["down_w"] = _np.transpose(_np.asarray(given["down_w"]), (2, 0, 1))
    given["router_w"] = _np.transpose(_np.asarray(given["router_w"]))
    given["up_w"] = _np.transpose(_np.asarray(given["up_w"]), (0, 2, 1))
    for name, array in {**given, **shape_constants()}.items():
        array = _np.ascontiguousarray(array)
        arrays[f"in_{name}"] = array
        args[name] = nc.dram_tensor(f"in_{name}", array.shape, _mybir.dt.from_np(array.dtype),
                                    kind="ExternalInput").ap()
    out = nc.dram_tensor("out_0", (B, T, E), F32, kind="ExternalOutput").ap()
    build(nc, args, out)
    r = _run(nc, [arrays], core_ids=[0])
    return r.results[0]["out_0"]
```
